# Optimizing a Trainium2 kernel written in Bass

```python
import numpy as np
import jax
import jax.numpy as jnp

def _softmax(x, axis=-1):
    return jax.nn.softmax(x, axis=axis)

def _gelu(x):
    return jax.nn.gelu(x, approximate=True)

def _silu(x):
    return jax.nn.silu(x)

def _sigmoid(x):
    return jax.nn.sigmoid(x)

def _layernorm(x, axis=-1, eps=1e-05):
    m = jnp.mean(x, axis=axis, keepdims=True)
    v = jnp.var(x, axis=axis, keepdims=True)
    return (x - m) / jnp.sqrt(v + eps)

def _scatter_add(tgt, idx, src, axis=0):
    return tgt.at[idx].add(src)

def _segment_sum(src, seg, n):
    return jax.ops.segment_sum(src, seg, n)
kernel_name = 'mk_decoder_postln_d1_seqx_r8_1d619e'

def setup_inputs(seed: int=0):
    np.random.seed(seed)
    _w = jnp.asarray

    def _rec_inputs():
        import jax
        import jax.numpy as jnp
        _rk = jax.random.key(seed)
        x = 7.22e-05 + 1 * jax.random.normal(jax.random.fold_in(_rk, 1), (4, 256, 128), jnp.float32)
        _lenS = 256 - jax.random.randint(jax.random.fold_in(_rk, 7), (4,), 0, max(1, 256 // 4) + 1, jnp.int32)
        _lenS2 = 256 - jax.random.randint(jax.random.fold_in(_rk, 8), (4,), 0, max(1, 256 // 4) + 1, jnp.int32)
        _ctx_1024P = jax.random.normal(jax.random.fold_in(_rk, 11), (4, 16, 128), jnp.float32)
        _ctx_1024c = jax.random.dirichlet(jax.random.fold_in(_rk, 511), 0.3 * jnp.ones((16,), jnp.float32), (4, 256))
        _ctx_1024t = jnp.einsum('bsk,bkd->bsd', _ctx_1024c, _ctx_1024P)
        _ctx_1024t = _ctx_1024t * jax.lax.rsqrt(jnp.mean(jnp.square(_ctx_1024t)) + 1e-12) * 0.953939
        ctx_1024 = 4.13588e-05 + 0.999923 * (_ctx_1024t + 0.3 * jax.random.normal(jax.random.fold_in(_rk, 611), (4, 256, 128), jnp.float32))
        return (x, ctx_1024)
    x, ctx_1024 = _rec_inputs()

    def _L0_attn_setup():
        import jax, jax.numpy as jnp
        import numpy as np
        B, S, D = (2, 256, 128)
        H = 16
        HD = D // H
        WINDOW = 128
        SCALE = HD ** (-0.5)

        def _local_mask(seq_len):
            idx = jnp.arange(seq_len)
            band = jnp.abs(idx[:, None] - idx[None, :]) <= WINDOW // 2
            return jnp.where(band, 0.0, -jnp.inf).astype(jnp.float32)
        key = jax.random.key(seed)
        ks = jax.random.split(key, 5)
        x = jax.random.normal(ks[0], (B, S, D), dtype=jnp.float32)
        w_qkv = jax.random.normal(ks[1], (D, 3 * D), dtype=jnp.float32) * D ** (-0.5)
        b_qkv = jax.random.normal(ks[2], (3 * D,), dtype=jnp.float32) * 0.02
        w_out = jax.random.normal(ks[3], (D, D), dtype=jnp.float32) * D ** (-0.5)
        b_out = jax.random.normal(ks[4], (D,), dtype=jnp.float32) * 0.02
        return {'x': x, 'w_qkv': w_qkv, 'b_qkv': b_qkv, 'w_out': w_out, 'b_out': b_out}
    _L0_attn_all = _L0_attn_setup()
    _L0_attn_in = {k: v for k, v in _L0_attn_all.items() if k in ('w_qkv', 'b_qkv', 'w_out', 'b_out')}
    del _L0_attn_all

    def _L0_xattn_setup():
        import jax, jax.numpy as jnp
        import numpy as np
        D_MODEL = 128
        NUM_HEADS = 16
        HEAD_DIM = D_MODEL // NUM_HEADS
        MAX_SEQ = 64

        def rope_tables(seq_len, dim):
            inv_freq = 1.0 / 10000.0 ** (jnp.arange(0, dim, 2, dtype=jnp.float32) / dim)
            t = jnp.arange(seq_len, dtype=jnp.float32)
            freqs = jnp.einsum('i,j->ij', t, inv_freq)
            emb = jnp.concatenate([freqs, freqs], axis=-1)
            return (jnp.cos(emb), jnp.sin(emb))

        def rotate_half(x):
            x1, x2 = jnp.split(x, 2, axis=-1)
            return jnp.concatenate([-x2, x1], axis=-1)
        key = jax.random.key(seed)
        ks = jax.random.split(key, 12)
        B, S, D = (16, 64, D_MODEL)
        s = 1.0 / np.sqrt(D)
        inp = {'query': jax.random.normal(ks[0], (B, S, D), jnp.float32), 'key': jax.random.normal(ks[1], (B, S, D), jnp.float32), 'value': jax.random.normal(ks[2], (B, S, D), jnp.float32), 'Wq': jax.random.normal(ks[3], (D, D), jnp.float32) * s, 'bq': jnp.zeros((D,), jnp.float32), 'Wk': jax.random.normal(ks[4], (D, D), jnp.float32) * s, 'bk': jnp.zeros((D,), jnp.float32), 'Wv': jax.random.normal(ks[5], (D, D), jnp.float32) * s, 'bv': jnp.zeros((D,), jnp.float32), 'Wo': jax.random.normal(ks[6], (D, D), jnp.float32) * s, 'bo': jnp.zeros((D,), jnp.float32)}
        return inp
    _L0_xattn_all = _L0_xattn_setup()
    _L0_xattn_in = {k: v for k, v in _L0_xattn_all.items() if k in ('Wq', 'bq', 'Wk', 'bk', 'Wv', 'bv', 'Wo', 'bo')}
    del _L0_xattn_all

    def _L0_ffn_setup():
        import jax, jax.numpy as jnp
        import numpy as np
        D_MODEL = 128
        N_EXPERTS = 16
        TOP_K = 2
        EXPERT_DIM = 128
        SHARED_DIM = 256
        B, T = (2, 128)
        key = jax.random.key(seed)
        ks = jax.random.split(key, 7)
        std = 0.02
        return {'x': jax.random.normal(ks[0], (B, T, D_MODEL), dtype=jnp.float32), 'router_w': jax.random.normal(ks[1], (N_EXPERTS, D_MODEL), dtype=jnp.float32) * std, 'gate_up_w': jax.random.normal(ks[2], (N_EXPERTS, D_MODEL, 2 * EXPERT_DIM), dtype=jnp.float32) * std, 'down_w': jax.random.normal(ks[3], (N_EXPERTS, EXPERT_DIM, D_MODEL), dtype=jnp.float32) * std, 'shared_gate_w': jax.random.normal(ks[4], (SHARED_DIM, D_MODEL), dtype=jnp.float32) * std, 'shared_up_w': jax.random.normal(ks[5], (SHARED_DIM, D_MODEL), dtype=jnp.float32) * std, 'shared_down_w': jax.random.normal(ks[6], (D_MODEL, SHARED_DIM), dtype=jnp.float32) * std}
    _L0_ffn_all = _L0_ffn_setup()
    _L0_ffn_in = {k: v for k, v in _L0_ffn_all.items() if k in ('router_w', 'gate_up_w', 'down_w', 'shared_gate_w', 'shared_up_w', 'shared_down_w')}
    del _L0_ffn_all
    return {'x': x, 'ctx_1024': ctx_1024, 'L0_attn_w_qkv': _L0_attn_in['w_qkv'], 'L0_attn_b_qkv': _L0_attn_in['b_qkv'], 'L0_attn_w_out': _L0_attn_in['w_out'], 'L0_attn_b_out': _L0_attn_in['b_out'], 'L0_xattn_Wq': _L0_xattn_in['Wq'], 'L0_xattn_bq': _L0_xattn_in['bq'], 'L0_xattn_Wk': _L0_xattn_in['Wk'], 'L0_xattn_bk': _L0_xattn_in['bk'], 'L0_xattn_Wv': _L0_xattn_in['Wv'], 'L0_xattn_bv': _L0_xattn_in['bv'], 'L0_xattn_Wo': _L0_xattn_in['Wo'], 'L0_xattn_bo': _L0_xattn_in['bo'], 'L0_ffn_router_w': _L0_ffn_in['router_w'], 'L0_ffn_gate_up_w': _L0_ffn_in['gate_up_w'], 'L0_ffn_down_w': _L0_ffn_in['down_w'], 'L0_ffn_shared_gate_w': _L0_ffn_in['shared_gate_w'], 'L0_ffn_shared_up_w': _L0_ffn_in['shared_up_w'], 'L0_ffn_shared_down_w': _L0_ffn_in['shared_down_w']}

def reference(x, ctx_1024, L0_attn_w_qkv, L0_attn_b_qkv, L0_attn_w_out, L0_attn_b_out, L0_xattn_Wq, L0_xattn_bq, L0_xattn_Wk, L0_xattn_bk, L0_xattn_Wv, L0_xattn_bv, L0_xattn_Wo, L0_xattn_bo, L0_ffn_router_w, L0_ffn_gate_up_w, L0_ffn_down_w, L0_ffn_shared_gate_w, L0_ffn_shared_up_w, L0_ffn_shared_down_w):
    import jax
    import jax.numpy as jnp

    def _L0_attn_ref(x, w_qkv, b_qkv, w_out, b_out):
        import jax, jax.numpy as jnp
        import numpy as np
        B, S, D = (2, 256, 128)
        H = 16
        HD = D // H
        WINDOW = 128
        SCALE = HD ** (-0.5)

        def _local_mask(seq_len):
            idx = jnp.arange(seq_len)
            band = jnp.abs(idx[:, None] - idx[None, :]) <= WINDOW // 2
            return jnp.where(band, 0.0, -jnp.inf).astype(jnp.float32)
        b, s, _ = x.shape
        qkv = x @ w_qkv + b_qkv
        qkv = qkv.reshape(b, s, 3, H, HD).transpose(2, 0, 3, 1, 4)
        q, k, v = (qkv[0], qkv[1], qkv[2])
        mask = _local_mask(s)
        scores = jnp.einsum('bhqd,bhkd->bhqk', q, k) * SCALE + mask
        attn = jax.nn.softmax(scores, axis=-1)
        out = jnp.einsum('bhqk,bhkd->bhqd', attn, v)
        out = out.transpose(0, 2, 1, 3).reshape(b, s, D)
        return out @ w_out + b_out

    def _L0_xattn_ref(query, key, value, Wq, bq, Wk, bk, Wv, bv, Wo, bo):
        import jax, jax.numpy as jnp
        import numpy as np
        D_MODEL = 128
        NUM_HEADS = 16
        HEAD_DIM = D_MODEL // NUM_HEADS
        MAX_SEQ = 64

        def rope_tables(seq_len, dim):
            inv_freq = 1.0 / 10000.0 ** (jnp.arange(0, dim, 2, dtype=jnp.float32) / dim)
            t = jnp.arange(seq_len, dtype=jnp.float32)
            freqs = jnp.einsum('i,j->ij', t, inv_freq)
            emb = jnp.concatenate([freqs, freqs], axis=-1)
            return (jnp.cos(emb), jnp.sin(emb))

        def rotate_half(x):
            x1, x2 = jnp.split(x, 2, axis=-1)
            return jnp.concatenate([-x2, x1], axis=-1)
        B, S, D = query.shape
        H, Hd = (NUM_HEADS, HEAD_DIM)
        scale = Hd ** (-0.5)

        def proj(x, W, b):
            y = jnp.einsum('bsd,ed->bse', x, W) + b
            return y.reshape(B, S, H, Hd).transpose(0, 2, 1, 3)
        q = proj(query, Wq, bq)
        k = proj(key, Wk, bk)
        v = proj(value, Wv, bv)
        cos, sin = rope_tables(S, Hd)
        cos = cos[None, None]
        sin = sin[None, None]
        q = q * cos + rotate_half(q) * sin
        k = k * cos + rotate_half(k) * sin
        attn = jnp.einsum('bhqd,bhkd->bhqk', q, k) * scale
        attn_w = jax.nn.softmax(attn, axis=-1)
        out = jnp.einsum('bhqk,bhkd->bhqd', attn_w, v)
        out = out.transpose(0, 2, 1, 3).reshape(B, S, D)
        out = jnp.einsum('bsd,ed->bse', out, Wo) + bo
        return out

    def _L0_ffn_ref(x, router_w, gate_up_w, down_w, shared_gate_w, shared_up_w, shared_down_w):
        import jax, jax.numpy as jnp
        import numpy as np
        D_MODEL = 128
        N_EXPERTS = 16
        TOP_K = 2
        EXPERT_DIM = 128
        SHARED_DIM = 256
        B, T = (2, 128)
        Bb, Tt, C = x.shape
        N = Bb * Tt
        E = gate_up_w.shape[0]
        logits = jnp.einsum('btc,ec->bte', x, router_w)
        top_vals, top_idx = jax.lax.top_k(logits, TOP_K)
        gates = jax.nn.sigmoid(top_vals)
        xf = x.reshape(N, C)
        sel = top_idx.reshape(N, TOP_K)
        gw = gates.reshape(N, TOP_K)
        w_full = jnp.zeros((N, E), dtype=x.dtype).at[jnp.arange(N)[:, None], sel].add(gw)
        gu = jnp.einsum('nc,ech->neh', xf, gate_up_w)
        gate, up = jnp.split(gu, 2, axis=-1)
        h = jax.nn.silu(gate) * up
        out_all = jnp.einsum('neh,ehc->nec', h, down_w)
        moe = jnp.einsum('ne,nec->nc', w_full, out_all).reshape(Bb, Tt, C)
        sg = jnp.einsum('btc,sc->bts', x, shared_gate_w)
        su = jnp.einsum('btc,sc->bts', x, shared_up_w)
        shared = jnp.einsum('bts,cs->btc', jax.nn.silu(sg) * su, shared_down_w)
        return moe + shared
    x = _layernorm(x + _L0_attn_ref(x, L0_attn_w_qkv, L0_attn_b_qkv, L0_attn_w_out, L0_attn_b_out), axis=-1)
    x = _layernorm(x + _L0_xattn_ref(x, ctx_1024, ctx_1024, L0_xattn_Wq, L0_xattn_bq, L0_xattn_Wk, L0_xattn_bk, L0_xattn_Wv, L0_xattn_bv, L0_xattn_Wo, L0_xattn_bo), axis=-1)
    x = _layernorm(x + _L0_ffn_ref(x, L0_ffn_router_w, L0_ffn_gate_up_w, L0_ffn_down_w, L0_ffn_shared_gate_w, L0_ffn_shared_up_w, L0_ffn_shared_down_w), axis=-1)
    return x

_drawn_inputs = setup_inputs


def setup_inputs(seed=0):
    import zlib

    import numpy as np

    out = dict(_drawn_inputs(seed))
    spreads = {'L0_xattn_bq': (0.0, 0.44),
     'L0_xattn_bk': (0.0, 0.8),
     'L0_xattn_bv': (0.0, 0.1),
     'L0_xattn_bo': (0.0, 0.1)}
    factors = {'L0_attn_b_qkv': 2.899,
     'L0_attn_b_out': 3.066,
     'L0_ffn_router_w': 8.0,
     'L0_ffn_gate_up_w': 8.0,
     'L0_ffn_down_w': 8.0,
     'L0_ffn_shared_gate_w': 6.973,
     'L0_ffn_shared_up_w': 6.757,
     'L0_ffn_shared_down_w': 6.748}
    for name, (base, spread) in spreads.items():
        noise = np.random.default_rng([zlib.crc32(name.encode()), seed]).standard_normal(out[name].shape)
        drawn = base * np.exp(spread * noise) if base else spread * noise
        out[name] = jnp.asarray(drawn.astype(out[name].dtype))
    for name, factor in factors.items():
        out[name] = (out[name] * factor).astype(out[name].dtype)
    return out
```

```python
from contextlib import ExitStack

import numpy as np

import concourse.bass as bass
from concourse import mybir

F32 = mybir.dt.float32
F32R = mybir.dt.float32r
BF16 = mybir.dt.bfloat16
U32 = mybir.dt.uint32
ALU = mybir.AluOpType
ACT = mybir.ActivationFunctionType
AX = mybir.AxisListType

B, S, D, H, HD = 4, 256, 128, 16, 8
WINDOW = 128
HALF = WINDOW // 2
N_TOK = B * S
P = 128
NT = S // P
E, TOP_K, F = 16, 2, 128
NSH = 2
NE = E + NSH
EPS = 1e-5
SCALE = float(HD) ** -0.5
BAND = P + HALF
MASKED = -1e30
NJ = 2 * B
NPART = 3
ZERO0, NM0 = 64, 96
KS_ROWS, KT_ROWS = 96, 99
AHEAD = 23
VW = 32
CH = 512
NC = N_TOK // CH
PT_RING, W_RING = 8, 6
DOWN_LAG = 3
H_RING = DOWN_LAG + 1
GU_CH = 2 * 2 * F
MOE0 = NJ * H
LAST = MOE0 + NC * NE + 8

BQ, BK, BV, XQ, XQS, XK, XKS, XV = range(8)
WQ, WQS, WK, WKS, WV, WO = range(6)


def is_local(j):
    return j < B


def tasks_at(n):
    out = []
    for j in range(NJ):
        at = {"q": -40, "q_hi": -39, "q_mid": -38, "v": -29} if is_local(j) else \
             {"k": -48, "k_hi": -46, "k_mid": -44, "v": -29, "q": -35, "q_hi": -34, "q_mid": -32}
        at.update({"stack": -31, "neg_max": H - AHEAD, "nm_turn": H - AHEAD + 2, "o_even": 10, "o_odd": 18,
                   "norm0": 20, "norm1": 21, "o_turn": 23, "proj": 25, "ln": 26, "y_turn": 28})
        if not is_local(j):
            at.update({"route": 30, "gates": 32, "w_turn": 35})
        if j == NJ - 1:
            at.update({"norm0": 19, "norm1": 20, "o_turn": 21, "proj": 22, "ln": 22, "y_turn": 23, "route": 24,
                       "gates": 24, "w_turn": 25})
        out += [(name, j) for name, d in at.items() if n == H * j + d]
    return out


STEPS = range(-48, LAST)
A_TASKS = [t for n in STEPS for t in tasks_at(n) if t[0] in ("q", "k", "v", "nm_turn")]
E_TASKS = [t for n in STEPS for t in tasks_at(n) if t[0] in ("norm0", "norm1", "o_turn", "proj", "y_turn", "route",
                                                             "w_turn")]


def expert_order(i):
    return (E + i) if i < NSH else i - NSH


def decoder_layer(nc, t, scratch_parts, scratch_w, out):
    ctx = ExitStack()
    with ctx:
        def sb(name, shape, dt=F32):
            return ctx.enter_context(nc.sbuf_tensor(name, shape, dt))

        def sem(name):
            return ctx.enter_context(nc.semaphore(name))

        def bank(name):
            return ctx.enter_context(nc.psum_tensor(name, [P, 512], F32))

        xT, ctxT = sb("xT", [P, N_TOK]), sb("ctxT", [P, N_TOK])
        x_tok = sb("x_tok", [P, B * NT, D])
        w_attn = sb("w_attn", [P, 4, D])
        w_cross = sb("w_cross", [P, 6, D])
        bias = sb("bias", [P, 8])
        out_bias = sb("out_bias", [P, 2, D])
        cos_t, sin_t = sb("cos_t", [P, S]), sb("sin_t", [P, S])
        ident = sb("ident", [P, P])
        ident_b = sb("ident_b", [P, P], BF16)
        band = sb("band", [P, NT * BAND], BF16)
        iota = sb("iota", [P, E])
        w_router = sb("w_router", [P, E])
        w_gu = sb("w_gu", [P, 2, GU_CH])
        w_gu_hi = sb("w_gu_hi", [P, NE * 2 * F], F32R)
        w_gu_lo = sb("w_gu_lo", [P, NE * 2 * F], F32R)
        w_down = sb("w_down", [P, NE, D])
        half_neg = sb("half_neg", [P, NT])

        full = [sb("q_full", [P, S]), sb("k_full", [P, S])]
        rope = [sb("q_rope", [P, 2, S]), sb("k_rope", [P, 2, S])]
        rest = [sb("q_rest", [P, S]), sb("k_rest", [P, S])]
        parts = [sb("q_parts", [P, NPART, S], BF16), sb("k_parts", [P, NPART, S], BF16)]
        q_stack = [sb(f"q_stack{i}", [P, H, S], BF16) for i in range(3)]
        k_stack = [sb(f"k_stack{i}", [P, H, S], BF16) for i in range(3)]
        v_ones = [sb(f"v_ones{i}", [P, NT, H, VW]) for i in range(3)]

        row_max = [sb(f"row_max{i}", [P, NT, H]) for i in range(2)]
        nm_rest = sb("nm_rest", [P, 2, NT, H])
        nm = sb("nm", [P, NT, NPART, H], BF16)
        nm_t = sb("nm_t", [NPART * H, S], BF16)
        probs = sb("probs", [P, PT_RING, NT * S])

        oT = sb("oT", [P, 4, S])
        denom = sb("denom", [P, H])
        o_tok = sb("o_tok", [P, NT, D])
        oT_n = sb("oT_n", [P, S])
        z = sb("z", [P, NT, D])
        stats, mean_var = sb("stats", [P, NT, 6]), sb("mean_var", [P, NT, 2])
        var_eps, rstd = sb("var_eps", [P, NT]), sb("rstd", [P, NT])
        y1, y1_res = sb("y1", [P, B * NT, D]), sb("y1_res", [P, B * NT, D])
        y1T = sb("y1T", [P, N_TOK])
        y2 = sb("y2", [P, B * NT, D])
        y2T = sb("y2T", [P, N_TOK])
        y2T_hi, y2T_lo = sb("y2T_hi", [P, N_TOK], F32R), sb("y2T_lo", [P, N_TOK], F32R)

        logits = sb("logits", [P, NT, E])
        top, top_at = sb("top", [P, NT, 8]), sb("top_at", [P, NT, 8], U32)
        top_f = sb("top_f", [P, NT, 8])
        gate_e, gate_s = sb("gate_e", [P, NT, TOP_K]), sb("gate_s", [P, NT, TOP_K])
        pick = sb("pick", [P, NT, E])
        w_full = sb("w_full", [P, NT, E])
        wT = sb("wT", [E, S])

        w_bc = probs[:, 0:W_RING, :]
        spare = q_stack[0][:, :, :].rearrange("p h s -> p (h s)").bitcast(F32).rearrange("p (a b c) -> p a b c",
                                                                                          a=2, b=2)
        silu, h_raw = spare[:, 0], spare[:, 1]
        h_w = sb("h_w", [P, H_RING, CH])
        spare = k_stack[0][:, 0:8, :].rearrange("p h s -> p (h s)").bitcast(F32).rearrange("p (a n d) -> p a n d",
                                                                                          a=2, d=D)
        z3, y3 = spare[:, 0], spare[:, 1]
        stats3, mean_var3 = sb("stats3", [P, 4, 6]), sb("mean_var3", [P, 4, 2])
        var_eps3, rstd3 = sb("var_eps3", [P, 4]), sb("rstd3", [P, 4])
        half_neg3 = sb("half_neg3", [P, 4])

        ps_s = [bank("ps_s0"), bank("ps_s1")]
        ps_t = [bank("ps_t0"), bank("ps_t1")]
        ps_o = [bank("ps_o0"), bank("ps_o1")]
        ps_a, ps_e = bank("ps_a"), bank("ps_e")

        ld_first, ld_cross, ld_tok = sem("ld_first"), sem("ld_cross"), sem("ld_tok")
        masks_ready = sem("masks_ready")
        ld_gu, ld_down = [sem("ld_gu0"), sem("ld_gu1")], sem("ld_down")
        rows_zero = [sem(f"rows_zero{i}") for i in range(3)]
        ones_fixed, cols_fixed = sem("ones_fixed"), sem("cols_fixed")
        res_ready = sem("res_ready")
        a_filled, e_filled = sem("a_filled"), sem("e_filled")
        roped = [sem("q_roped"), sem("k_roped")]
        full_ready = [sem("q_full_ready"), sem("k_full_ready")]
        hi_ready = [sem("q_hi"), sem("k_hi")]
        rest_ready = [sem("q_rest_ready"), sem("k_rest_ready")]
        mid_ready = [sem("q_mid_ready"), sem("k_mid_ready")]
        lo_ready = [sem("q_lo"), sem("k_lo")]
        scr_written = [sem("q_scr"), sem("k_scr")]
        stacked = [[sem(f"{x}_stacked{i}") for i in range(3)] for x in "qk"]
        v_ready = sem("v_ready")
        s_scored, max_ready = sem("s_scored"), sem("max_ready")
        nm_ready, nm_turned = sem("nm_ready"), sem("nm_turned")
        nm_stacked = [sem(f"nm_stacked{i}") for i in range(2)]
        t_scored, exp_done = sem("t_scored"), sem("exp_done")
        pv_done, o_out = sem("pv_done"), sem("o_out")
        o_norm, o_turned, z_ready = sem("o_norm"), sem("o_turned"), sem("z_ready")
        var_ready, rstd_ready, y_ready = sem("var_ready"), sem("rstd_ready"), sem("y_ready")
        yT_ready, y2_split = sem("yT_ready"), sem("y2_split")
        y1_res_ready = sem("y1_res_ready")
        logits_ready = sem("logits_ready")
        top_ready, gate_exp, w_ready, wT_ready = sem("top_ready"), sem("gate_exp"), sem("w_ready"), sem("wT_ready")
        w_scr = sem("w_scr")
        w_bc_ready = [sem(f"w_bc_ready{i}") for i in range(W_RING)]
        gu_split = sem("gu_split")
        gu_done, silu_done, h_ready, down_done = sem("gu_done"), sem("silu_done"), sem("h_ready"), sem("down_done")
        var3_ready, rstd3_ready, y3_ready = sem("var3_ready"), sem("rstd3_ready"), sem("y3_ready")
        stored = sem("stored")
        dve_step = sem("dve_step")
        pool_step = sem("pool_step")

        def tok(b):
            return slice(b * S, (b + 1) * S)

        def a_turn(name, j):
            return A_TASKS.index((name, j))

        def e_turn(name, j):
            return E_TASKS.index((name, j))

        def q_cols(j, kt):
            return (HALF * kt, BAND) if is_local(j) else (0, S)

        def routed(m):
            return (m // NE) * E + max(0, m % NE - NSH)

        def zero_rows(stack):
            return stack[ZERO0:96, :, :].bitcast(U32)

        block = ctx.enter_context(nc.Block())

        @block.sync
        def _(sp):
            sp.dma_start(w_attn[:, 0:2], t["w_attn"][:, 0:2]).then_inc(ld_first, 16)
            sp.dma_start(xT[:, tok(0)], t["xT"][:, tok(0)]).then_inc(ld_first, 16)
            sp.dma_start(bias[:], t["bias"]).then_inc(ld_first, 16)
            sp.dma_start(w_attn[:, 2:4], t["w_attn"][:, 2:4]).then_inc(ld_first, 16)
            sp.dma_start(xT[:, S:N_TOK], t["xT"][:, S:N_TOK]).then_inc(ld_tok, 16)
            sp.dma_start(x_tok[:], t["x"].rearrange("(n p) d -> p n d", p=P)).then_inc(ld_tok, 16)
            sp.dma_start(out_bias[:], t["out_bias"].partition_broadcast(P)).then_inc(ld_tok, 16)

            def write_parts(side, j):
                sp.wait_ge(lo_ready[side], j + 1)
                sp.wait_ge(mid_ready[side], j + 1)
                sp.dma_start(scratch_parts[j, side].rearrange("a p t -> p a t"),
                             parts[side][:, :, :]).then_inc(scr_written[side], 16)

            def read_stack(side, j):
                if j >= 3:
                    sp.wait_ge(t_scored, H * (j - 2))
                else:
                    sp.wait_ge(rows_zero[j], 1)
                sp.wait_ge(scr_written[side], 16 * (j + 1))
                src = scratch_parts[j, side].rearrange("a (d h) t -> a d (h t)", d=HD)
                dst = (q_stack, k_stack)[side][j % 3][0:NPART * NPART * HD].rearrange("p h t -> p (h t)")
                if side == 0:
                    sp.dma_start(dst, src.rearrange("a d n -> (a d) n").partition_broadcast(NPART)
                                 ).then_inc(stacked[side][j % 3], 16)
                else:
                    for b in range(NPART):
                        rows = NPART * HD
                        sp.dma_start(dst[rows * b:rows * (b + 1)], src[b].partition_broadcast(NPART)
                                     ).then_inc(stacked[side][j % 3], 16)

            for n in STEPS:
                for name, j in tasks_at(n):
                    if name == "q_mid":
                        write_parts(0, j)
                        if is_local(j):
                            write_parts(1, j)
                    if name == "k_mid":
                        write_parts(1, j)
                    if name == "stack":
                        read_stack(1, j)
                        read_stack(0, j)
                    if name == "stack" and j == 0:
                        sp.dma_start(w_cross[:], t["w_cross"]).then_inc(ld_cross, 16)
                        sp.dma_start(ctxT[:], t["ctxT"]).then_inc(ld_cross, 16)
                        sp.dma_start(cos_t[:], t["cos"]).then_inc(ld_cross, 16)
                        sp.dma_start(sin_t[:], t["sin"]).then_inc(ld_cross, 16)
                        sp.dma_start(w_down[:], t["w_down"]).then_inc(ld_down, 16)
                        sp.dma_start(w_router[:], t["w_router"]).then_inc(ld_down, 16)
                        sp.dma_start(iota[:], t["iota"]).then_inc(ld_down, 16)
                if n % 8 == 2 and 0 <= n // 8 < NE // 2:
                    k = n // 8
                    if k >= 2:
                        sp.wait_ge(gu_split, 2 * (k - 1))
                    sp.dma_start(w_gu[:, k % 2, :], t["w_gu"][:, k * GU_CH:(k + 1) * GU_CH]).then_inc(ld_gu[k % 2], 16)
                if n == MOE0:
                    sp.wait_ge(pv_done, 4 * NJ)
                if n >= MOE0:
                    for m in (range(4) if n == MOE0 else [n - MOE0 + 3]):
                        if m >= NC * NE or m % NE < NSH:
                            continue
                        r = routed(m)
                        c = m // NE
                        sp.wait_ge(w_scr, 16 * 2 * (c + 1))
                        if r >= W_RING:
                            prev = r - W_RING
                            sp.wait_ge(h_ready, (prev // E) * NE + prev % E + NSH + 1)
                        sp.dma_start(w_bc[:, r % W_RING, :],
                                     scratch_w[expert_order(m % NE), c * CH:(c + 1) * CH].partition_broadcast(P)
                                     ).then_inc(w_bc_ready[r % W_RING], 16)
                    for c in range(NC):
                        if n == MOE0 + NE * (c + 1) + DOWN_LAG + 4:
                            sp.wait_ge(y3_ready, c + 1)
                            sp.dma_start(out[c * CH:(c + 1) * CH, :].rearrange("(n p) d -> p n d", p=P),
                                         y3[:]).then_inc(stored, 16)
            sp.wait_ge(stored, 16 * NC)

        @block.tensor
        def _(pe):
            def first_scores(j, i):
                unit = H * j + i
                qt, pair = i // 8, i % 8
                k0, width = q_cols(j, qt)
                dst = ps_s[unit % 2]
                if i == 0:
                    pe.wait_ge(stacked[0][j % 3], 16 * (j // 3 + 1))
                    pe.wait_ge(stacked[1][j % 3], 16 * NPART * (j // 3 + 1))
                if unit >= 2:
                    pe.wait_ge(max_ready, unit - 1)
                if is_local(j):
                    if unit == 0:
                        pe.wait_ge(masks_ready, 3)
                    pe.matmul(dst[:, 0:2 * width],
                              ident_b[:, :],
                              band[:, qt * BAND:(qt + 1) * BAND].unsqueeze(1).to_broadcast([P, 2, BAND]),
                              start=True, stop=False, skip_group_check=True)
                for k in range(2):
                    h = 2 * pair + k
                    last = pe.matmul(dst[:, k * width:(k + 1) * width],
                                     q_stack[j % 3][0:KS_ROWS, h, qt * P:(qt + 1) * P],
                                     k_stack[j % 3][0:KS_ROWS, h, k0:k0 + width],
                                     start=not is_local(j), stop=True, skip_group_check=True)
                last.then_inc(s_scored, 1)

            def second_scores(j, h):
                unit = H * j + h
                dst = ps_t[unit % 2]
                if h == 0:
                    pe.wait_ge(nm_stacked[j % 2], 16 * (j // 2 + 1))
                    if j < 3:
                        pe.wait_ge(ones_fixed, j + 1)
                if unit >= 2:
                    pe.wait_ge(exp_done, unit - 1)
                width = q_cols(j, 0)[1]
                if is_local(j):
                    pe.matmul(dst[:, 0:NT * width], ident_b[:, :], band[:, :], start=True, stop=False,
                              skip_group_check=True)
                for kt in range(NT):
                    q0 = q_cols(j, kt)[0]
                    last = pe.matmul(dst[:, kt * width:(kt + 1) * width],
                                     k_stack[j % 3][0:KT_ROWS, h, kt * P:(kt + 1) * P],
                                     q_stack[j % 3][0:KT_ROWS, h, q0:q0 + width],
                                     start=not is_local(j), stop=True, skip_group_check=True)
                last.then_inc(t_scored, 1)

            def weigh_values(j, g):
                pe.wait_ge(exp_done, H * j + 4 * g + 4)
                if g == 0:
                    pe.wait_ge(v_ready, j + 1)
                if g % 2 == 0 and j >= 1:
                    pe.wait_ge(o_out, 2 * (j - 1) + g // 2 + 1)
                for kt in range(NT):
                    q0, width = q_cols(j, kt)
                    for c in range(4):
                        h = 4 * g + c
                        col = (g % 2) * S + q0
                        last = pe.matmul(ps_o[g // 2][32 * c:32 * c + VW, col:col + width],
                                         v_ones[j % 3][:, kt, h, :],
                                         probs[:, (H * j + h) % PT_RING, kt * width:(kt + 1) * width],
                                         start=(kt == 0), stop=(kt == NT - 1), skip_group_check=True)
                last.then_inc(pv_done, 1)

            def turn_a(name, j):
                k = a_turn(name, j)
                if k:
                    last, i = A_TASKS[k - 1]
                    if last == "q" and is_local(i):
                        pe.wait_ge(full_ready[1], i + 1)
                    elif last == "q":
                        pe.wait_ge(roped[0], i - B + 1)
                    elif last == "k":
                        pe.wait_ge(roped[1], i - B + 1)
                    elif last == "v":
                        pe.wait_ge(v_ready, i + 1)
                    else:
                        pe.wait_ge(nm_turned, i + 1)

            def turn_e(name, j):
                k = e_turn(name, j)
                if k:
                    last, i = E_TASKS[k - 1]
                    if last in ("norm0", "norm1"):
                        pe.wait_ge(o_norm, 2 * i + int(last[-1]) + 1)
                    elif last == "o_turn":
                        pe.wait_ge(o_turned, i + 1)
                    elif last == "proj":
                        pe.wait_ge(z_ready, i + 1)
                    elif last == "y_turn" and is_local(i):
                        pe.wait_ge(yT_ready, i + 1)
                    elif last == "y_turn":
                        pe.wait_ge(y2_split, i - B + 1)
                    elif last == "route":
                        pe.wait_ge(logits_ready, i - B + 1)
                    else:
                        pe.wait_ge(wT_ready, i - B + 1)

            def task(name, j):
                b = j % B
                if name in ("q", "k"):
                    turn_a(name, j)
                    if is_local(j):
                        if j == 0:
                            pe.wait_ge(ld_first, 64)
                        if j == 1:
                            pe.wait_ge(ld_tok, 48)
                        pairs = [(w_attn[:, 0, :], xT), (w_attn[:, 1, :], xT)]
                    elif name == "q":
                        pe.wait_ge(yT_ready, b + 1)
                        pairs = [(w_cross[:, WQ, :], y1T), (w_cross[:, WQS, :], y1T)]
                    else:
                        pe.wait_ge(ld_cross, 64)
                        pairs = [(w_cross[:, WK, :], ctxT), (w_cross[:, WKS, :], ctxT)]
                    for k, (w, src) in enumerate(pairs):
                        last = pe.matmul(ps_a[:, k * S:(k + 1) * S], w, src[:, tok(b)], start=True, stop=True)
                    last.then_inc(a_filled, 1)
                elif name == "v":
                    turn_a(name, j)
                    src, w = (xT, w_attn[:, 2, :]) if is_local(j) else (ctxT, w_cross[:, WV, :])
                    for kt in range(NT):
                        at = b * S + kt * P
                        last = pe.matmul(ps_a[:, kt * D:(kt + 1) * D], src[:, at:at + P], w, start=True, stop=True)
                    last.then_inc(a_filled, 1)
                elif name == "nm_turn":
                    turn_a(name, j)
                    pe.wait_ge(nm_ready, j + 1)
                    for qt in range(NT):
                        last = pe.transpose(ps_a[0:NPART * H, :].bitcast(BF16)[:, qt * P:(qt + 1) * P],
                                            nm[:, qt].rearrange("p a h -> p (a h)"), ident_b[:, :])
                    last.then_inc(a_filled, 1)
                elif name in ("norm0", "norm1"):
                    turn_e(name, j)
                    qt = int(name[-1])
                    pe.wait_ge(o_out, 2 * j + 2)
                    for g in range(4):
                        last = pe.transpose(ps_e[:, g * P:(g + 1) * P], oT[:, g, qt * P:(qt + 1) * P], ident[:, :])
                    last.then_inc(e_filled, 1)
                elif name == "o_turn":
                    turn_e(name, j)
                    for qt in range(NT):
                        last = pe.transpose(ps_e[:, qt * P:(qt + 1) * P], o_tok[:, qt, :], ident[:, :])
                    last.then_inc(e_filled, 1)
                elif name == "proj":
                    turn_e(name, j)
                    w = w_attn[:, 3, :] if is_local(j) else w_cross[:, WO, :]
                    for qt in range(NT):
                        last = pe.matmul(ps_e[:, qt * D:(qt + 1) * D], oT_n[:, qt * P:(qt + 1) * P], w,
                                         start=True, stop=True)
                    last.then_inc(e_filled, 1)
                elif name == "y_turn":
                    turn_e(name, j)
                    pe.wait_ge(y_ready, j + 1)
                    y = y1 if is_local(j) else y2
                    for qt in range(NT):
                        last = pe.transpose(ps_e[:, qt * P:(qt + 1) * P], y[:, b * NT + qt, :], ident[:, :])
                    last.then_inc(e_filled, 1)
                elif name == "route":
                    turn_e(name, j)
                    pe.wait_ge(yT_ready, j + 1)
                    if j == B:
                        pe.wait_ge(ld_down, 48)
                    for qt in range(NT):
                        at = b * S + qt * P
                        last = pe.matmul(ps_e[:, qt * E:(qt + 1) * E], y2T[:, at:at + P], w_router[:, :],
                                         start=True, stop=True)
                    last.then_inc(e_filled, 1)
                elif name == "w_turn":
                    turn_e(name, j)
                    pe.wait_ge(w_ready, b + 1)
                    for qt in range(NT):
                        last = pe.transpose(ps_e[0:E, qt * P:(qt + 1) * P], w_full[:, qt, :], ident[:, :])
                    last.then_inc(e_filled, 1)

            def gate_up(m):
                c, e = m // NE, expert_order(m % NE)
                banks = (ps_s[m % 2], ps_t[m % 2])
                if m == 0:
                    pe.wait_ge(gu_split, 2 * NE // 2)
                    pe.wait_ge(max_ready, NJ * H)
                    pe.wait_ge(exp_done, NJ * H)
                if m % NE == 0:
                    pe.wait_ge(y2_split, 2 * (c + 1))
                if m >= 2:
                    pe.wait_ge(h_ready, m - 1)
                for k, dst in enumerate(banks):
                    col = (2 * e + k) * F
                    for i, (w, y) in enumerate(((w_gu_hi, y2T_hi), (w_gu_hi, y2T_lo), (w_gu_lo, y2T_hi))):
                        last = pe.matmul(dst[:, :], w[:, col:col + F], y[:, c * CH:(c + 1) * CH],
                                         start=(i == 0), stop=(i == 2))
                last.then_inc(gu_done, 1)

            def down(m):
                c, e = m // NE, expert_order(m % NE)
                pe.wait_ge(h_ready, m + 1)
                if m == 0:
                    pe.wait_ge(ld_down, 48)
                if m % NE == 0:
                    pe.wait_ge(o_out, 2 * NJ)
                for k in range(CH // P):
                    last = pe.matmul(ps_o[c][:, k * D:(k + 1) * D], h_w[:, m % H_RING, k * P:(k + 1) * P], w_down[:, e, :],
                                     start=(m % NE == 0 and k == 0), stop=(m % NE == NE - 1),
                                     skip_group_check=True)
                last.then_inc(down_done, 1)

            for n in STEPS:
                if 0 <= n < MOE0:
                    second_scores(n // H, n % H)
                if 0 <= n + AHEAD < MOE0:
                    first_scores((n + AHEAD) // H, (n + AHEAD) % H)
                k = n - 6
                if k >= 0 and k % 4 == 0 and k // 4 < 4 * NJ:
                    weigh_values(k // 16, k // 4 % 4)
                for name, j in tasks_at(n):
                    task(name, j)
                m = n - MOE0
                if 0 <= m < NC * NE:
                    gate_up(m)
                if DOWN_LAG <= m < NC * NE + DOWN_LAG:
                    down(m - DOWN_LAG)

        @block.vector
        def _(dve):
            chain = [0]

            def link(ins):
                chain[0] += 1
                ins.then_inc(dve_step, 1)
                dve.wait_ge(dve_step, chain[0])

            dve.memset(zero_rows(q_stack[0]), 0)
            dve.memset(zero_rows(k_stack[0]), 0).then_inc(rows_zero[0], 1)
            for i in range(3):
                dve.memset(k_stack[i][NM0:KT_ROWS, :, :].bitcast(U32), 0x3F803F80).then_inc(ones_fixed, 1)

            def maxima(j, i):
                unit = H * j + i
                qt, pair = i // 8, i % 8
                width = q_cols(j, 0)[1]
                dve.wait_ge(s_scored, unit + 1)
                if i == 0 and j >= 2:
                    dve.wait_ge(nm_ready, j - 1)
                dve.tensor_reduce(row_max[j % 2][:, qt, 2 * pair:2 * pair + 2],
                                  ps_s[unit % 2][:, 0:2 * width].rearrange("p (k w) -> p k w", k=2),
                                  AX.X, ALU.max).then_inc(max_ready, 1)

            def rope_side(side, j):
                b0 = (XQ, XK)[side]
                if side == 1:
                    dve.wait_ge(a_filled, a_turn("k", j) + 1)
                else:
                    dve.wait_ge(a_filled, a_turn("q", j) + 1)
                if j > B:
                    dve.wait_ge(full_ready[side], j)
                if j == B:
                    dve.wait_ge(ld_cross, 64)
                dve.scalar_tensor_tensor(rope[side][:, 0, :], ps_a[:, 0:S], bias[:, b0:b0 + 1], cos_t[:, :],
                                         ALU.add, ALU.mult)
                dve.scalar_tensor_tensor(rope[side][:, 1, :], ps_a[:, S:2 * S], bias[:, b0 + 1:b0 + 2], sin_t[:, :],
                                         ALU.add, ALU.mult).then_inc(roped[side], 1)

            def layer_norm_stats(src, st, mv, ve, tiles, ready):
                for k in range(tiles):
                    last = dve.bn_stats(st[:, k, :], src[:, k, :])
                link(last)
                for k in range(tiles):
                    last = dve.bn_aggr(mv[:, k, :], st[:, k, :])
                link(last)
                dve.tensor_scalar(ve[:, :], mv[:, :, 1], EPS, None, ALU.add).then_inc(ready, 1)

            def task(name, j):
                b = j % B
                if name == "q" and not is_local(j):
                    rope_side(0, j)
                if name == "k":
                    rope_side(1, j)
                if name == "neg_max":
                    dve.wait_ge(max_ready, H * (j + 1))
                    if j >= 1:
                        dve.wait_ge(a_filled, a_turn("nm_turn", j - 1) + 1)
                    m = row_max[j % 2]
                    link(dve.tensor_scalar(nm[:, :, 0, :], m[:, :, :], -1.0, None, ALU.mult))
                    link(dve.scalar_tensor_tensor(nm_rest[:, 0], m[:, :, :], -1.0, nm[:, :, 0, :],
                                                  ALU.mult, ALU.subtract))
                    link(dve.tensor_copy(nm[:, :, 1, :], nm_rest[:, 0]))
                    dve.tensor_tensor(nm[:, :, 2, :], nm_rest[:, 0], nm[:, :, 1, :],
                                      ALU.subtract).then_inc(nm_ready, 1)
                if name in ("norm0", "norm1"):
                    qt = int(name[-1])
                    dve.wait_ge(e_filled, e_turn(name, j) + 1)
                    o = ps_e[:, :].rearrange("p (h c) -> p h c", c=VW)
                    link(dve.reciprocal(denom[:, :], o[:, :, HD]))
                    ins = dve.tensor_tensor(o_tok[:, qt, :].rearrange("p (h c) -> p h c", c=HD), o[:, :, 0:HD],
                                            denom[:, :].unsqueeze(2).to_broadcast([P, H, HD]), ALU.mult)
                    ins.then_inc(o_norm, 1)
                if name == "proj":
                    dve.wait_ge(e_filled, e_turn(name, j) + 1)
                    if is_local(j):
                        dve.wait_ge(res_ready, 1)
                        res = x_tok
                    else:
                        dve.wait_ge(y1_res_ready, b + 1)
                        res = y1_res
                    ins = dve.tensor_tensor(z[:, :, :].rearrange("p n d -> p (n d)"), ps_e[:, 0:NT * D],
                                            res[:, b * NT:(b + 1) * NT, :].rearrange("p n d -> p (n d)"), ALU.add)
                    ins.then_inc(z_ready, 1)
                    dve.wait_ge(z_ready, j + 1)
                    layer_norm_stats(z, stats, mean_var, var_eps, NT, var_ready)
                if name == "ln":
                    dve.wait_ge(rstd_ready, j + 1)
                    y = y1 if is_local(j) else y2
                    for k in range(NT):
                        last = dve.tensor_scalar(y[:, b * NT + k, :], z[:, k, :], mean_var[:, k, 0:1],
                                                 rstd[:, k:k + 1], ALU.subtract, ALU.mult)
                    last.then_inc(y_ready, 1)
                    dve.wait_ge(y_ready, j + 1)
                if name == "y_turn" and not is_local(j):
                    dve.wait_ge(yT_ready, j + 1)
                    dve.tensor_tensor(y2T_lo[:, tok(b)], ps_e[:, 0:S], y2T_hi[:, tok(b)].bitcast(F32),
                                      ALU.subtract).then_inc(y2_split, 1)
                if name == "route":
                    dve.wait_ge(e_filled, e_turn(name, j) + 1)
                    ins = dve.tensor_copy(logits[:, :, :].rearrange("p n e -> p (n e)"), ps_e[:, 0:NT * E])
                    ins.then_inc(logits_ready, 1)
                    dve.wait_ge(logits_ready, b + 1)
                    for k in range(NT):
                        last = dve.max(top[:, k, :], logits[:, k, :])
                    last.then_inc(top_ready, 1)
                    dve.wait_ge(top_ready, b + 1)
                    for k in range(NT):
                        last = dve.max_index(top_at[:, k, :], top[:, k, :], logits[:, k, :])
                    link(last)
                    link(dve.tensor_copy(top_f[:, :, :], top_at[:, :, :]))
                if name == "gates":
                    dve.wait_ge(gate_exp, b + 1)
                    link(dve.tensor_scalar(gate_s[:, :, :], gate_e[:, :, :], 1.0, None, ALU.add))
                    link(dve.reciprocal(gate_s[:, :, :], gate_s[:, :, :]))
                    for k in range(NT):
                        last = dve.tensor_scalar(pick[:, k, :], iota[:, :], top_f[:, k, 0:1], gate_s[:, k, 0:1],
                                                 ALU.is_equal, ALU.mult)
                    link(last)
                    if b >= 1:
                        dve.wait_ge(e_filled, e_turn("w_turn", j - 1) + 1)
                    for k in range(NT):
                        last = dve.tensor_scalar(w_full[:, k, :], iota[:, :], top_f[:, k, 1:2], gate_s[:, k, 1:2],
                                                 ALU.is_equal, ALU.mult)
                    link(last)
                    dve.tensor_tensor(w_full[:, :, :], w_full[:, :, :], pick[:, :, :], ALU.add).then_inc(w_ready, 1)

            def hidden(m):
                c, e = m // NE, expert_order(m % NE)
                dve.wait_ge(silu_done, m + 1)
                if m >= H_RING:
                    dve.wait_ge(down_done, m - H_RING + 1)
                dst = h_raw[:, m % 2, :] if e < E else h_w[:, m % H_RING, :]
                ins = dve.tensor_tensor(dst, silu[:, m % 2, :], ps_t[m % 2][:, :], ALU.mult)
                if e < E:
                    link(ins)
                    r = routed(m)
                    dve.wait_ge(w_bc_ready[r % W_RING], 16 * (r // W_RING + 1))
                    ins = dve.tensor_tensor(h_w[:, m % H_RING, :], h_raw[:, m % 2, :], w_bc[:, r % W_RING, :], ALU.mult)
                ins.then_inc(h_ready, 1)

            def last_norm_stats(c):
                dve.wait_ge(down_done, NE * (c + 1))
                if c:
                    dve.wait_ge(y3_ready, c)
                link(dve.tensor_tensor(z3[:, :, :].rearrange("p n d -> p (n d)"), ps_o[c][:, :],
                                       y2[:, 4 * c:4 * c + 4, :].rearrange("p n d -> p (n d)"), ALU.add))
                layer_norm_stats(z3, stats3, mean_var3, var_eps3, 4, var3_ready)

            def last_norm(c):
                dve.wait_ge(rstd3_ready, c + 1)
                if c:
                    dve.wait_ge(stored, 16 * c)
                for k in range(4):
                    last = dve.tensor_scalar(y3[:, k, :], z3[:, k, :], mean_var3[:, k, 0:1], rstd3[:, k:k + 1],
                                             ALU.subtract, ALU.mult)
                last.then_inc(y3_ready, 1)

            for n in STEPS:
                if 0 <= n + AHEAD < MOE0:
                    maxima((n + AHEAD) // H, (n + AHEAD) % H)
                for name, j in tasks_at(n):
                    task(name, j)
                m = n - MOE0
                if 0 <= m < NC * NE:
                    hidden(m)
                for c in range(NC):
                    if m == NE * (c + 1) + DOWN_LAG:
                        last_norm_stats(c)
                    if m == NE * (c + 1) + DOWN_LAG + 1:
                        last_norm(c)

        @block.scalar
        def _(act):
            for i in (1, 2):
                act.memzero(zero_rows(q_stack[i]))
                act.memzero(zero_rows(k_stack[i])).then_inc(rows_zero[i], 1)

            def exponentials(j, h):
                unit = H * j + h
                width = NT * q_cols(j, 0)[1]
                act.wait_ge(t_scored, unit + 1)
                if unit >= PT_RING:
                    act.wait_ge(pv_done, (unit - PT_RING) // 4 + 1)
                act.activation(probs[:, unit % PT_RING, 0:width], ps_t[unit % 2][:, 0:width], ACT.Exp,
                               scale=SCALE).then_inc(exp_done, 1)

            def hi_part(side, j):
                act.wait_ge(full_ready[side], j + 1)
                if j:
                    act.wait_ge(scr_written[side], 16 * j)
                act.activation(parts[side][:, 0, :], full[side][:, :], ACT.Copy).then_inc(hi_ready[side], 1)

            def mid_part(side, j):
                act.wait_ge(rest_ready[side], j + 1)
                act.activation(parts[side][:, 1, :], rest[side][:, :], ACT.Copy).then_inc(mid_ready[side], 1)

            def task(name, j):
                b = j % B
                if name == "q" and is_local(j):
                    act.wait_ge(a_filled, a_turn(name, j) + 1)
                    for side in (0, 1):
                        if j:
                            act.wait_ge(rest_ready[side], j)
                        ins = act.activation(full[side][:, :], ps_a[:, side * S:(side + 1) * S], ACT.Identity,
                                             bias=bias[:, BQ + side:BQ + side + 1])
                        ins.then_inc(full_ready[side], 1)
                if name == "q_hi":
                    for side in ((0, 1) if is_local(j) else (0,)):
                        hi_part(side, j)
                if name == "k_hi":
                    hi_part(1, j)
                if name == "q_mid":
                    for side in ((0, 1) if is_local(j) else (0,)):
                        mid_part(side, j)
                if name == "k_mid":
                    mid_part(1, j)
                if name == "v":
                    act.wait_ge(a_filled, a_turn(name, j) + 1)
                    if j < 3:
                        act.wait_ge(cols_fixed, j + 1)
                    else:
                        act.wait_ge(pv_done, 4 * (j - 2))
                    act.activation(v_ones[j % 3][:, :, :, 0:HD],
                                   ps_a[:, 0:NT * D].rearrange("p (n h c) -> p n h c", n=NT, c=HD),
                                   ACT.Copy).then_inc(v_ready, 1)
                if name == "nm_turn":
                    act.wait_ge(a_filled, a_turn(name, j) + 1)
                    if j:
                        act.wait_ge(nm_stacked[(j - 1) % 2], 16 * ((j - 1) // 2 + 1))
                    act.activation(nm_t[:, :], ps_a[0:NPART * H, :].bitcast(BF16)[:, 0:S],
                                   ACT.Copy).then_inc(nm_turned, 1)
                    act.wait_ge(nm_turned, j + 1)
                    if j >= 3:
                        act.wait_ge(t_scored, H * (j - 2))
                    act.dma_start(q_stack[j % 3][NM0:KT_ROWS, :, :], nm_t[:, :]).then_inc(nm_stacked[j % 2], 16)
                if name in ("o_even", "o_odd"):
                    k = int(name == "o_odd")
                    act.wait_ge(pv_done, 4 * j + 2 * k + 2)
                    if j and k == 0:
                        act.wait_ge(e_filled, e_turn("norm1", j - 1) + 1)
                    act.activation(oT[:, 2 * k:2 * k + 2, :].rearrange("p g s -> p (g s)"), ps_o[k][:, :],
                                   ACT.Copy).then_inc(o_out, 1)
                if name == "o_turn":
                    act.wait_ge(e_filled, e_turn(name, j) + 1)
                    col = BV if is_local(j) else XV
                    act.activation(oT_n[:, :], ps_e[:, 0:S], ACT.Identity,
                                   bias=bias[:, col:col + 1]).then_inc(o_turned, 1)
                if name == "y_turn":
                    act.wait_ge(e_filled, e_turn(name, j) + 1)
                    if is_local(j):
                        act.activation(y1T[:, tok(b)], ps_e[:, 0:S], ACT.Copy).then_inc(yT_ready, 1)
                    else:
                        act.activation(y2T[:, tok(b)], ps_e[:, 0:S], ACT.Copy)
                        act.activation(y2T_hi[:, tok(b)], ps_e[:, 0:S], ACT.Copy).then_inc(yT_ready, 1)
                if name == "route":
                    act.wait_ge(top_ready, b + 1)
                    act.activation(gate_e[:, :, :], top[:, :, 0:TOP_K], ACT.Exp, scale=-1.0).then_inc(gate_exp, 1)
                if name == "w_turn":
                    act.wait_ge(e_filled, e_turn(name, j) + 1)
                    if b:
                        act.wait_ge(w_scr, 16 * b)
                    act.activation(wT[:, :], ps_e[0:E, 0:S], ACT.Copy).then_inc(wT_ready, 1)
                    act.wait_ge(wT_ready, b + 1)
                    act.dma_start(scratch_w[:, tok(b)], wT[:]).then_inc(w_scr, 16)

            def gate(m):
                act.wait_ge(gu_done, m + 1)
                if m == 0:
                    act.wait_ge(t_scored, NJ * H)
                if m >= 2:
                    act.wait_ge(h_ready, m - 1)
                act.activation(silu[:, m % 2, :], ps_s[m % 2][:, :], ACT.Silu).then_inc(silu_done, 1)

            for n in STEPS:
                if 0 <= n < MOE0:
                    exponentials(n // H, n % H)
                for name, j in tasks_at(n):
                    task(name, j)
                if 0 <= n - MOE0 < NC * NE:
                    gate(n - MOE0)

        @block.gpsimd
        def _(pool):
            for m in (ident_b, ident):
                pool.memset(m[:], 0.0).then_inc(pool_step, 1)
            pool.memset(band[:], 0.0).then_inc(pool_step, 1)
            pool.wait_ge(pool_step, 3)
            for m in (ident_b, ident):
                pool.affine_select(out=m[:], in_=m[:], compare_op=ALU.not_equal, fill=1.0, base=0,
                                   pattern=[[-1, P]], channel_multiplier=1).then_inc(masks_ready, 1)
            for k in range(NT):
                cols = band[:, k * BAND:(k + 1) * BAND]
                pool.affine_select(out=cols, in_=cols, compare_op=ALU.is_ge, fill=MASKED, base=HALF * (k + 1),
                                   pattern=[[-1, BAND]], channel_multiplier=1).then_inc(pool_step, 1)
            pool.wait_ge(pool_step, 5)
            for k in range(NT):
                cols = band[:, k * BAND:(k + 1) * BAND]
                last = pool.affine_select(out=cols, in_=cols, compare_op=ALU.is_ge, fill=MASKED,
                                          base=HALF * (1 - k), pattern=[[1, BAND]], channel_multiplier=-1)
            last.then_inc(masks_ready, 1)
            pool.memset(half_neg[:], -0.5)
            pool.memset(half_neg3[:], -0.5).then_inc(pool_step, 1)
            for i in range(3):
                pool.memset(v_ones[i][:, :, :, HD + 1:VW], 0.0)
                pool.memset(v_ones[i][:, :, :, HD:HD + 1], 1.0).then_inc(cols_fixed, 1)

            def split(side, j):
                pool.wait_ge(hi_ready[side], j + 1)
                if j:
                    pool.wait_ge(lo_ready[side], j)
                    pool.wait_ge(mid_ready[side], j)
                pool.tensor_tensor(rest[side][:, :], full[side][:, :], parts[side][:, 0, :],
                                   ALU.subtract).then_inc(rest_ready[side], 1)

            def lo_part(side, j):
                pool.wait_ge(mid_ready[side], j + 1)
                pool.wait_ge(rest_ready[side], j + 1)
                pool.tensor_tensor(parts[side][:, 2, :], rest[side][:, :], parts[side][:, 1, :],
                                   ALU.subtract).then_inc(lo_ready[side], 1)

            def sum_rope(side, j):
                pool.wait_ge(roped[side], j - B + 1)
                if j:
                    pool.wait_ge(rest_ready[side], j)
                pool.tensor_tensor(full[side][:, :], rope[side][:, 0, :], rope[side][:, 1, :],
                                   ALU.add).then_inc(full_ready[side], 1)

            def task(name, j):
                b = j % B
                if name == "q" and not is_local(j):
                    sum_rope(0, j)
                if name == "k":
                    sum_rope(1, j)
                if name == "q_hi":
                    for side in ((0, 1) if is_local(j) else (0,)):
                        split(side, j)
                if name == "k_hi":
                    split(1, j)
                if name == "q_mid":
                    for side in ((0, 1) if is_local(j) else (0,)):
                        lo_part(side, j)
                if name == "k_mid":
                    lo_part(1, j)
                if name == "proj":
                    pool.wait_ge(var_ready, j + 1)
                    if j:
                        pool.wait_ge(y_ready, j)
                    pool.tensor_tensor(rstd[:, :], var_eps[:, :], half_neg[:, :], ALU.pow).then_inc(rstd_ready, 1)
                if name == "y_turn" and is_local(j):
                    pool.wait_ge(y_ready, j + 1)
                    pool.tensor_tensor(y1_res[:, b * NT:(b + 1) * NT, :], y1[:, b * NT:(b + 1) * NT, :],
                                       out_bias[:, 1, :].unsqueeze(1).to_broadcast([P, NT, D]),
                                       ALU.add).then_inc(y1_res_ready, 1)

            def split_weights(k):
                cols = slice(k * GU_CH, (k + 1) * GU_CH)
                pool.wait_ge(ld_gu[k % 2], 16 * (k // 2 + 1))
                pool.tensor_scalar(w_gu_hi[:, cols], w_gu[:, k % 2, :], 1.0, 0.0, ALU.mult,
                                   ALU.add).then_inc(gu_split, 1)
                pool.wait_ge(gu_split, 2 * k + 1)
                pool.tensor_tensor(w_gu_lo[:, cols], w_gu[:, k % 2, :], w_gu_hi[:, cols].bitcast(F32),
                                   ALU.subtract).then_inc(gu_split, 1)

            for n in STEPS:
                if n == -20:
                    pool.wait_ge(ld_tok, 48)
                    pool.tensor_tensor(x_tok[:, :, :], x_tok[:, :, :],
                                       out_bias[:, 0, :].unsqueeze(1).to_broadcast([P, B * NT, D]),
                                       ALU.add).then_inc(res_ready, 1)
                    pool.wait_ge(pool_step, 6)
                for name, j in tasks_at(n):
                    task(name, j)
                if n >= 4 and n % 8 == 4 and n // 8 < NE // 2:
                    split_weights(n // 8)
                for c in range(NC):
                    if n == MOE0 + NE * (c + 1) + DOWN_LAG:
                        pool.wait_ge(var3_ready, c + 1)
                        if c:
                            pool.wait_ge(y3_ready, c)
                        pool.tensor_tensor(rstd3[:, :], var_eps3[:, :], half_neg3[:, :],
                                           ALU.pow).then_inc(rstd3_ready, 1)


def _layouts(inp):
    c = np.ascontiguousarray

    def by_dim(w):
        return w.reshape(w.shape[:-1] + (H, HD)).swapaxes(-1, -2).reshape(w.shape)

    def swap_halves(w):
        s = w.shape
        return by_dim(w.reshape(s[:-1] + (H, 2, HD // 2))[..., ::-1, :].reshape(s))

    x = inp["x"].reshape(N_TOK, D)
    wq, wk, wv, wo = (inp[f"L0_xattn_W{n}"].T for n in "qkvo")
    bq, bk, bv = (inp[f"L0_xattn_b{n}"] for n in "qkv")
    bqkv = inp["L0_attn_b_qkv"]
    wqkv = inp["L0_attn_w_qkv"].reshape(D, 3, D)
    gu = np.concatenate([
        inp["L0_ffn_gate_up_w"].transpose(1, 0, 2).reshape(D, E * 2 * F),
        np.stack([inp["L0_ffn_shared_gate_w"].reshape(NSH, F, D), inp["L0_ffn_shared_up_w"].reshape(NSH, F, D)],
                 axis=1).transpose(3, 0, 1, 2).reshape(D, NSH * 2 * F)], axis=1)
    down = np.concatenate([
        inp["L0_ffn_down_w"].transpose(1, 0, 2),
        inp["L0_ffn_shared_down_w"].T.reshape(NSH, F, D).transpose(1, 0, 2)], axis=1)
    return {
        "x": c(x), "xT": c(x.T), "ctxT": c(inp["ctx_1024"].reshape(N_TOK, D).T),
        "w_attn": c(np.stack([by_dim(wqkv[:, 0]), by_dim(wqkv[:, 1]), wqkv[:, 2], inp["L0_attn_w_out"]], axis=1)),
        "w_cross": c(np.stack([by_dim(wq), swap_halves(wq), by_dim(wk), swap_halves(wk), wv, wo], axis=1)),
        "bias": c(np.stack([by_dim(bqkv[0:D]), by_dim(bqkv[D:2 * D]), bqkv[2 * D:], by_dim(bq), swap_halves(bq),
                            by_dim(bk), swap_halves(bk), bv], axis=1)),
        "out_bias": c(np.stack([inp["L0_attn_b_out"], inp["L0_xattn_bo"]])),
        "w_router": c(inp["L0_ffn_router_w"].T), "w_gu": c(gu), "w_down": c(down),
    }


def _tables():
    inv_freq = (1.0 / 10000.0 ** (np.arange(0, HD, 2, dtype=np.float32) / np.float32(HD))).astype(np.float32)
    angle = np.arange(S, dtype=np.float32)[None, :] * inv_freq[:, None]
    cos, sin = np.cos(angle).astype(np.float32), np.sin(angle).astype(np.float32)
    return {
        "cos": np.repeat(np.concatenate([cos, cos]), H, axis=0),
        "sin": np.repeat(np.concatenate([-sin, sin]), H, axis=0),
        "iota": np.tile(np.arange(E, dtype=np.float32), (P, 1)),
    }


def kernel(**inputs):
    import concourse.bacc as _bacc
    from concourse import mybir as _mybir
    from concourse.bass_utils import run_bass_kernel_spmd as _run

    arrays = {**_layouts({k: np.asarray(v) for k, v in inputs.items()}), **_tables()}
    nc = _bacc.Bacc("TRN2", target_bir_lowering=False, num_devices=1)
    t = {n: nc.dram_tensor(n + "_dram", a.shape, _mybir.dt.from_np(a.dtype), kind="ExternalInput").ap()
         for n, a in arrays.items()}
    scratch_parts = nc.dram_tensor("scratch_parts", [NJ, 2, NPART, P, S], _mybir.dt.bfloat16).ap()
    scratch_w = nc.dram_tensor("scratch_w", [E, N_TOK], _mybir.dt.float32).ap()
    out = nc.dram_tensor("out_dram", [N_TOK, D], _mybir.dt.float32, kind="ExternalOutput").ap()
    decoder_layer(nc, t, scratch_parts, scratch_w, out)
    r = _run(nc, [{n + "_dram": a for n, a in arrays.items()}], core_ids=[0])
    return r.results[0]["out_dram"].reshape(B, S, D)
```

```python
from contextlib import ExitStack

import numpy as np

import concourse.bass as bass
from concourse import mybir

F32 = mybir.dt.float32
F32R = mybir.dt.float32r
BF16 = mybir.dt.bfloat16
U32 = mybir.dt.uint32
ALU = mybir.AluOpType
ACT = mybir.ActivationFunctionType
AX = mybir.AxisListType

B, S, D, H, HD = 4, 256, 128, 16, 8
WINDOW = 128
HALF = WINDOW // 2
N_TOK = B * S
P = 128
NT = S // P
E, TOP_K, F = 16, 2, 128
NSH = 2
NE = E + NSH
EPS = 1e-5
SCALE = float(HD) ** -0.5
BAND = P + HALF
MASKED = -1e30
NJ = 2 * B
NPART = 3
ZERO0, NM0 = 64, 96
KS_ROWS, KT_ROWS = 96, 99
AHEAD = 22
VW = 32
CH = S
CT = CH // P
NC = N_TOK // CH
PT_RING, W_RING = 8, 9
SPLIT0, SPLIT_STEP = 68, 4
POOL_OF_4 = 2
BAND_LAG = 1
W_AHEAD = 8
DOWN_LAG = 6
H_RING = 5
HI_LAG = 2
LO_LAG = 2
LOW_BY_POOL = 9
FULL_RING = 4
GU_CH = 2 * 2 * F
MOE0 = NJ * H
EARLY0, EARLY_STEP, EARLY = 105, 1, 23
LAST = MOE0 + NC * NE - EARLY + 12

BQ, BK, BV, XQ, XQS, XK, XKS, XV = range(8)
WQ, WQS, WK, WKS, WV, WO = range(6)


def is_local(j):
    return j < B


LOCAL_AT = {"q": -42, "q_hi": -39, "q_mid": -36, "stack": -31, "v": -28, "neg_max": -6, "nm_turn": -4, "o_even": 14,
            "o_odd": 18, "norm0": 20, "norm1": 22, "o_turn": 24, "proj": 26, "ln": 27, "y_turn": 29}
CROSS_AT = {"k": -48, "k_hi": -45, "k_mid": -42, "q": -34, "q_hi": -33, "q_mid": -32, "stack": -32, "v": -29,
            "neg_max": -7, "nm_turn": -6, "o_even": 13, "o_odd": 18, "norm0": 20, "norm1": 22, "o_turn": 24,
            "proj": 26, "ln": 28, "y_turn": 30, "route": 31, "gates": 33, "w_turn": 35}
LAST_AT = {"o_odd": 16, "norm0": 17, "norm1": 20, "o_turn": 21, "proj": 22, "ln": 25, "y_turn": 26, "route": 28,
           "gates": 36, "w_turn": 41}
MOVED = {("act", "cross", "o_even"): 1, ("act", "cross", "route"): 1, ("act", "last", "o_odd"): 1,
         ("act", "last", "q_hi"): -1, ("dve", "last", "gates"): -1, ("dve", "last", "ln"): -1,
         ("dve", "last", "norm1"): -1}
PV_LAG = 6
WARM = 16


def tasks_at(n, engine="pe"):
    out = []
    for j in range(NJ):
        at = {**(LOCAL_AT if is_local(j) else CROSS_AT), **(LAST_AT if j == NJ - 1 else {})}
        kind = "last" if j == NJ - 1 else "local" if is_local(j) else "cross"
        out += [(name, j) for name, d in at.items() if n == H * j + d + MOVED.get((engine, kind, name), 0)]
    return out


STEPS = range(-48, LAST)
A_TASKS = [t for n in STEPS for t in tasks_at(n) if t[0] in ("q", "k", "v", "nm_turn")]
K_ORDER = [j for n in STEPS for name, j in tasks_at(n) if name == ("q" if is_local(j) else "k")]
E_TASKS = [t for n in STEPS for t in tasks_at(n) if t[0] in ("norm0", "norm1", "o_turn", "proj", "y_turn", "route",
                                                             "w_turn")]


def unit_step(m):
    return EARLY0 + EARLY_STEP * m if m < EARLY else MOE0 + m - EARLY


def unit_at(n):
    found = [m for m in range(EARLY) if unit_step(m) == n] if n < MOE0 else [n - MOE0 + EARLY]
    return found[0] if found else None


def weigh_step(g):
    return 4 * g + PV_LAG if g < 4 * NJ - 1 else MOE0


def pool_bands(pair):
    return pair % 4 < POOL_OF_4


def bands_by_pool(pairs):
    return sum(pool_bands(pair) for pair in range(pairs))


TANH_LAST = 127


def expert_order(i):
    return (E + i) if i < NSH else i - NSH


def decoder_layer(nc, t, scratch_parts, scratch_w, out):
    ctx = ExitStack()
    with ctx:
        def sb(name, shape, dt=F32):
            return ctx.enter_context(nc.sbuf_tensor(name, shape, dt))

        def sem(name):
            return ctx.enter_context(nc.semaphore(name))

        def bank(name):
            return ctx.enter_context(nc.psum_tensor(name, [P, 512], F32))

        xT, ctxT = sb("xT", [P, N_TOK]), sb("ctxT", [P, N_TOK])
        x_tok = sb("x_tok", [P, B * NT, D])
        w_attn = sb("w_attn", [P, 4, D])
        w_cross = sb("w_cross", [P, 6, D])
        bias = sb("bias", [P, 8])
        out_bias = sb("out_bias", [P, 2, D])
        cos_t, sin_t = sb("cos_t", [P, S]), sb("sin_t", [P, S])
        ident = sb("ident", [P, P])
        ident_b = sb("ident_b", [P, P], BF16)
        band = sb("band", [P, NT * BAND], BF16)
        iota = sb("iota", [P, E])
        w_router = sb("w_router", [P, E])
        w_gu = sb("w_gu", [P, 2, GU_CH])
        w_gu_hi = sb("w_gu_hi", [P, NE * 2 * F], F32R)
        w_gu_lo = sb("w_gu_lo", [P, NE * 2 * F], F32R)
        w_down = sb("w_down", [P, 2, 2, D])
        w_down_hi, w_down_lo = sb("w_down_hi", [P, NE, D], F32R), sb("w_down_lo", [P, NE, D], F32R)
        half_neg = sb("half_neg", [P, NT])

        full = [sb("q_full", [P, S]), sb("k_full", [P, S])]
        rope = [sb("q_rope", [P, 2, S]), sb("k_rope", [P, 2, S])]
        rest = [sb("q_rest", [P, S]), sb("k_rest", [P, S])]
        parts = [sb("q_parts", [P, NPART, S], BF16), sb("k_parts", [P, NPART, S], BF16)]
        q_stack = [sb(f"q_stack{i}", [P, H, S], BF16) for i in range(3)]
        k_stack = [sb(f"k_stack{i}", [P, H, S], BF16) for i in range(3)]
        v_ones = [sb(f"v_ones{i}", [P, NT, H, VW]) for i in range(3)]

        row_max = [sb(f"row_max{i}", [P, NT, H]) for i in range(2)]
        nm_rest = sb("nm_rest", [P, 2, NT, H])
        nm = sb("nm", [P, NT, NPART, H], BF16)
        nm_t = sb("nm_t", [NPART * H, S], BF16)
        probs = sb("probs", [P, PT_RING, NT * S])

        oT = sb("oT", [P, 4, S])
        denom = sb("denom", [P, H])
        o_tok = sb("o_tok", [P, NT, D])
        oT_n = sb("oT_n", [P, S])
        z = sb("z", [P, NT, D])
        stats, mean_var = sb("stats", [P, NT, 6]), sb("mean_var", [P, NT, 2])
        var_eps, rstd = sb("var_eps", [P, NT]), sb("rstd", [P, NT])
        y1 = x_tok
        y1_res = xT[:, :].rearrange("p (n d) -> p n d", d=D)
        y1T = sb("y1T", [P, N_TOK])
        y2 = ctxT[:, :].rearrange("p (n d) -> p n d", d=D)
        y2T = y1T
        y2T_hi, y2T_lo = sb("y2T_hi", [P, N_TOK], F32R), sb("y2T_lo", [P, N_TOK], F32R)

        logits = sb("logits", [P, NT, E])
        top, top_at = sb("top", [P, NT, 8]), sb("top_at", [P, NT, 8], U32)
        top_f = sb("top_f", [P, NT, 8])
        gate_e, gate_s = sb("gate_e", [P, NT, TOP_K]), sb("gate_s", [P, NT, TOP_K])
        pick = sb("pick", [P, NT, E])
        w_full = sb("w_full", [P, NT, E])
        wT = sb("wT", [E, S])

        w_bc = [stack[:, h:h + 2, :].rearrange("p h s -> p (h s)").bitcast(F32)
                for stack, first in ((q_stack[2], 8), (k_stack[2], 4)) for h in range(first, H, 2)]
        downT = w_bc.pop()
        spare = q_stack[2][:, 0:8, :].rearrange("p h s -> p (h s)").bitcast(F32).rearrange("p (a b c) -> p a b c",
                                                                                          a=2, b=2)
        silu, h_raw = spare[:, 0], spare[:, 1]
        h_full = sb("h_full", [P, FULL_RING, CH])
        h_hi, h_lo = sb("h_hi", [P, H_RING, CH], F32R), sb("h_lo", [P, H_RING, CH], F32R)
        spare = k_stack[2][:, 0:4, :].rearrange("p h s -> p (h s)").bitcast(F32).rearrange("p (a n d) -> p a n d",
                                                                                          a=2, d=D)
        z3, y3 = spare[:, 0], spare[:, 1]
        stats3, mean_var3 = sb("stats3", [P, CT, 6]), sb("mean_var3", [P, CT, 2])
        var_eps3, rstd3 = sb("var_eps3", [P, CT]), sb("rstd3", [P, CT])
        half_neg3 = sb("half_neg3", [P, CT])

        ps_s = [bank("ps_s0"), bank("ps_s1")]
        ps_t = [bank("ps_t0"), bank("ps_t1")]
        ps_o = [bank("ps_o0"), bank("ps_o1")]
        ps_a, ps_e = bank("ps_a"), bank("ps_e")

        ld_first, ld_v, ld_cross, ld_tok = sem("ld_first"), sem("ld_v"), sem("ld_cross"), sem("ld_tok")
        masks_ready = sem("masks_ready")
        ld_gu, ld_route = [sem("ld_gu0"), sem("ld_gu1")], sem("ld_route")
        rows_zero = [sem(f"rows_zero{i}") for i in range(3)]
        ones_fixed, cols_fixed = sem("ones_fixed"), sem("cols_fixed")
        res_ready = sem("res_ready")
        a_filled, e_filled = sem("a_filled"), sem("e_filled")
        roped = [sem("q_roped"), sem("k_roped")]
        full_ready = [sem("q_full_ready"), sem("k_full_ready")]
        hi_ready = [sem("q_hi"), sem("k_hi")]
        rest_ready = [sem("q_rest_ready"), sem("k_rest_ready")]
        mid_ready = [sem("q_mid_ready"), sem("k_mid_ready")]
        lo_ready = [sem("q_lo"), sem("k_lo")]
        scr_written = [sem("q_scr"), sem("k_scr")]
        stacked = [[sem(f"{x}_stacked{i}") for i in range(3)] for x in "qk"]
        v_ready = sem("v_ready")
        s_scored, max_ready = sem("s_scored"), sem("max_ready")
        nm_ready, nm_turned = sem("nm_ready"), sem("nm_turned")
        nm_stacked = [sem(f"nm_stacked{i}") for i in range(2)]
        t_scored, exp_done = sem("t_scored"), sem("exp_done")
        banded = sem("banded")
        pv_done, o_out = sem("pv_done"), sem("o_out")
        o_norm, o_turned, z_ready = sem("o_norm"), sem("o_turned"), sem("z_ready")
        var_ready, rstd_ready, y_ready = sem("var_ready"), sem("rstd_ready"), sem("y_ready")
        yT_ready, y2_split = sem("yT_ready"), sem("y2_split")
        y1_res_ready = sem("y1_res_ready")
        logits_ready = sem("logits_ready")
        top_ready, gate_exp, w_ready, wT_ready = sem("top_ready"), sem("gate_exp"), sem("w_ready"), sem("wT_ready")
        w_scr = sem("w_scr")
        w_bc_ready = [sem(f"w_bc_ready{i}") for i in range(W_RING)]
        gu_split = sem("gu_split")
        gu_done, silu_done, gu_read = sem("gu_done"), sem("silu_done"), sem("gu_read")
        h_ready, down_done = sem("h_ready"), sem("down_done")
        h_hi_ready, h_lo_ready = sem("h_hi_ready"), sem("h_lo_ready")
        down_split = sem("down_split")
        down_out_T, down_turned = sem("down_out_T"), sem("down_turned")
        var3_ready, rstd3_ready, y3_ready = sem("var3_ready"), sem("rstd3_ready"), sem("y3_ready")
        stored = sem("stored")
        dve_step = sem("dve_step")
        pool_step = sem("pool_step")

        def tok(b):
            return slice(b * S, (b + 1) * S)

        def a_turn(name, j):
            return A_TASKS.index((name, j))

        def e_turn(name, j):
            return E_TASKS.index((name, j))

        def turn_of(side, j):
            return K_ORDER.index(j) if side else j

        def sides_with_q(j):
            return (0, 1) if is_local(j) and j else (0,)

        def q_cols(j, kt):
            return (HALF * kt, BAND) if is_local(j) else (0, S)

        def routed(m):
            return (m // NE) * E + max(0, m % NE - NSH)

        def gu_bank(m):
            return ps_s[m % 2] if m < EARLY else (ps_t + ps_s)[(m - EARLY) % 4]

        def bank_before(m):
            before = [k for k in range(m) if gu_bank(k) is gu_bank(m)]
            return before[-1] if before else None

        def gate_up_of(m):
            return gu_bank(m)[:, 0:CH], gu_bank(m)[:, CH:2 * CH]

        def down_out(c):
            return (ps_a, ps_o[0], ps_o[1], ps_a)[c][:, 0:CT * D]

        def zero_rows(stack):
            return stack[ZERO0:96, :, :].bitcast(U32)

        block = ctx.enter_context(nc.Block())

        @block.sync
        def _(sp):
            sp.dma_start(w_attn[:, 0:2], t["w_attn"][:, 0:2]).then_inc(ld_first, 16)
            sp.dma_start(xT[:, tok(0)], t["xT"][:, tok(0)]).then_inc(ld_first, 16)
            sp.dma_start(bias[:], t["bias"]).then_inc(ld_first, 16)
            sp.dma_start(w_attn[:, 2:4], t["w_attn"][:, 2:4]).then_inc(ld_v, 16)
            sp.dma_start(xT[:, S:N_TOK], t["xT"][:, S:N_TOK]).then_inc(ld_tok, 16)
            sp.dma_start(x_tok[:], t["x"].rearrange("(n p) d -> p n d", p=P)).then_inc(ld_tok, 16)
            sp.dma_start(out_bias[:], t["out_bias"].partition_broadcast(P)).then_inc(ld_tok, 16)

            def write_parts(side, j):
                sp.wait_ge(lo_ready[side], turn_of(side, j) + 1)
                sp.wait_ge(mid_ready[side], turn_of(side, j) + 1)
                sp.dma_start(scratch_parts[j, side].rearrange("a p t -> p a t"),
                             parts[side][:, :, :]).then_inc(scr_written[side], 16)

            def read_stack(side, j):
                if j >= 3:
                    sp.wait_ge(t_scored, H * (j - 2))
                else:
                    sp.wait_ge(rows_zero[j], 1)
                sp.wait_ge(scr_written[side], 16 * (turn_of(side, j) + 1))
                src = scratch_parts[j, side].rearrange("a (d h) t -> a d (h t)", d=HD)
                dst = (q_stack, k_stack)[side][j % 3][0:NPART * NPART * HD].rearrange("p h t -> p (h t)")
                if side == 0:
                    sp.dma_start(dst, src.rearrange("a d n -> (a d) n").partition_broadcast(NPART)
                                 ).then_inc(stacked[side][j % 3], 16)
                else:
                    for b in range(NPART):
                        rows = NPART * HD
                        sp.dma_start(dst[rows * b:rows * (b + 1)], src[b].partition_broadcast(NPART)
                                     ).then_inc(stacked[side][j % 3], 16)

            for n in STEPS:
                for name, j in tasks_at(n, "sp"):
                    if name == "q_mid":
                        if is_local(j):
                            write_parts(1, j)
                        write_parts(0, j)
                    if name == "k_mid":
                        write_parts(1, j)
                    if name == "stack":
                        read_stack(1, j)
                        read_stack(0, j)
                    if name == "stack" and j == 1:
                        sp.dma_start(w_cross[:], t["w_cross"]).then_inc(ld_cross, 16)
                        sp.dma_start(ctxT[:], t["ctxT"]).then_inc(ld_cross, 16)
                        sp.dma_start(cos_t[:], t["cos"]).then_inc(ld_cross, 16)
                        sp.dma_start(sin_t[:], t["sin"]).then_inc(ld_cross, 16)
                        sp.dma_start(w_router[:], t["w_router"]).then_inc(ld_route, 16)
                        sp.dma_start(iota[:], t["iota"]).then_inc(ld_route, 16)
                for k in range(NE // 2):
                    if n == SPLIT0 + SPLIT_STEP * (k - 2) + 1:
                        if k >= 2:
                            sp.wait_ge(gu_split, 2 * (k - 1))
                            sp.wait_ge(down_split, 2 * (k - 1))
                        sp.dma_start(w_gu[:, k % 2, :],
                                     t["w_gu"][:, k * GU_CH:(k + 1) * GU_CH]).then_inc(ld_gu[k % 2], 16)
                        sp.dma_start(w_down[:, k % 2], t["w_down"][:, 2 * k:2 * k + 2]).then_inc(ld_gu[k % 2], 16)
                unit = unit_at(n)
                if unit is not None:
                    for m in (range(W_AHEAD) if unit == 0 else [unit + W_AHEAD - 1]):
                        if m >= NC * NE or m % NE < NSH:
                            continue
                        r = routed(m)
                        c = m // NE
                        sp.wait_ge(w_scr, 16 * (c + 1))
                        if r == 0:
                            sp.wait_ge(t_scored, H * (NJ - 2))
                        if r >= W_RING:
                            prev = r - W_RING
                            sp.wait_ge(h_ready, prev + 1)
                        sp.dma_start(w_bc[r % W_RING],
                                     scratch_w[expert_order(m % NE), c * CH:(c + 1) * CH].partition_broadcast(P)
                                     ).then_inc(w_bc_ready[r % W_RING], 16)
                    for c in range(NC):
                        if unit == NE * (c + 1) + DOWN_LAG + 5:
                            sp.wait_ge(y3_ready, c + 1)
                            sp.dma_start(out[c * CH:(c + 1) * CH, :].rearrange("(n p) d -> p n d", p=P),
                                         y3[:]).then_inc(stored, 16)
            sp.wait_ge(stored, 16 * NC)

        @block.tensor
        def _(pe):
            def first_scores(j, i):
                unit = H * j + i
                qt, pair = i // 8, i % 8
                k0, width = q_cols(j, qt)
                dst = ps_s[unit % 2]
                if i == 0:
                    pe.wait_ge(stacked[0][j % 3], 16 * (j // 3 + 1))
                    pe.wait_ge(stacked[1][j % 3], 16 * NPART * (j // 3 + 1))
                if unit >= 2:
                    pe.wait_ge(max_ready, unit - 1)
                if is_local(j):
                    if unit == 0:
                        pe.wait_ge(masks_ready, 3)
                    pe.matmul(dst[:, 0:2 * width],
                              ident_b[:, :],
                              band[:, qt * BAND:(qt + 1) * BAND].unsqueeze(1).to_broadcast([P, 2, BAND]),
                              start=True, stop=False, skip_group_check=True)
                for k in range(2):
                    h = 2 * pair + k
                    last = pe.matmul(dst[:, k * width:(k + 1) * width],
                                     q_stack[j % 3][0:KS_ROWS, h, qt * P:(qt + 1) * P],
                                     k_stack[j % 3][0:KS_ROWS, h, k0:k0 + width],
                                     start=not is_local(j), stop=True, skip_group_check=True)
                last.then_inc(s_scored, 1)

            def second_scores(j, h):
                unit = H * j + h
                dst = ps_t[unit % 2]
                if h == 0:
                    pe.wait_ge(nm_stacked[j % 2], 16 * (j // 2 + 1))
                    if j < 3:
                        pe.wait_ge(ones_fixed, j + 1)
                if unit >= 2:
                    pe.wait_ge(exp_done, unit - 1)
                width = q_cols(j, 0)[1]
                on_band = is_local(j) and not pool_bands(unit // 2)
                if on_band:
                    pe.matmul(dst[:, 0:NT * width], ident_b[:, :], band[:, :], start=True, stop=False,
                              skip_group_check=True)
                for kt in range(NT):
                    q0 = q_cols(j, kt)[0]
                    last = pe.matmul(dst[:, kt * width:(kt + 1) * width],
                                     k_stack[j % 3][0:KT_ROWS, h, kt * P:(kt + 1) * P],
                                     q_stack[j % 3][0:KT_ROWS, h, q0:q0 + width],
                                     start=not on_band, stop=True, skip_group_check=True)
                last.then_inc(t_scored, 1)

            def weigh_values(j, g):
                pe.wait_ge(exp_done, H * j + 4 * g + 4)
                if is_local(j) and bands_by_pool(2 * (4 * j + g) + 2):
                    pe.wait_ge(banded, bands_by_pool(2 * (4 * j + g) + 2))
                if g == 0:
                    pe.wait_ge(v_ready, j + 1)
                if g % 2 == 0 and j >= 1:
                    pe.wait_ge(o_out, 2 * (j - 1) + g // 2 + 1)
                for kt in range(NT):
                    q0, width = q_cols(j, kt)
                    for c in range(4):
                        h = 4 * g + c
                        col = (g % 2) * S + q0
                        last = pe.matmul(ps_o[g // 2][32 * c:32 * c + VW, col:col + width],
                                         v_ones[j % 3][:, kt, h, :],
                                         probs[:, (H * j + h) % PT_RING, kt * width:(kt + 1) * width],
                                         start=(kt == 0), stop=(kt == NT - 1), skip_group_check=True)
                last.then_inc(pv_done, 1)

            def turn_a(name, j):
                k = a_turn(name, j)
                if k:
                    last, i = A_TASKS[k - 1]
                    if last == "q" and is_local(i):
                        pe.wait_ge(full_ready[0], i + 1)
                        pe.wait_ge(full_ready[1], turn_of(1, i) + 1)
                    elif last == "q":
                        pe.wait_ge(roped[0], i - B + 1)
                    elif last == "k":
                        pe.wait_ge(roped[1], i - B + 1)
                    elif last == "v":
                        pe.wait_ge(v_ready, i + 1)
                    else:
                        pe.wait_ge(nm_turned, i + 1)

            def turn_e(name, j):
                k = e_turn(name, j)
                if k:
                    last, i = E_TASKS[k - 1]
                    if last in ("norm0", "norm1"):
                        pe.wait_ge(o_norm, 2 * i + int(last[-1]) + 1)
                    elif last == "o_turn":
                        pe.wait_ge(o_turned, i + 1)
                    elif last == "proj":
                        pe.wait_ge(z_ready, i + 1)
                    elif last == "y_turn" and is_local(i):
                        pe.wait_ge(yT_ready, i + 1)
                    elif last == "y_turn":
                        pe.wait_ge(y2_split, i - B + 1)
                    elif last == "route":
                        pe.wait_ge(logits_ready, i - B + 1)
                    else:
                        pe.wait_ge(wT_ready, i - B + 1)

            def task(name, j):
                b = j % B
                if name in ("q", "k"):
                    turn_a(name, j)
                    if is_local(j):
                        if j == 0:
                            pe.wait_ge(ld_first, 48)
                        if j == 1:
                            pe.wait_ge(ld_tok, 48)
                        pairs = [(w_attn[:, 0, :], xT), (w_attn[:, 1, :], xT)]
                    elif name == "q":
                        pe.wait_ge(yT_ready, b + 1)
                        pairs = [(w_cross[:, WQ, :], y1T), (w_cross[:, WQS, :], y1T)]
                    else:
                        pe.wait_ge(ld_cross, 64)
                        pairs = [(w_cross[:, WK, :], ctxT), (w_cross[:, WKS, :], ctxT)]
                    for k, (w, src) in enumerate(pairs):
                        dst = ps_o[0][:, 0:S] if k and j == 0 else ps_a[:, k * S:(k + 1) * S]
                        last = pe.matmul(dst, w, src[:, tok(b)], start=True, stop=True)
                    last.then_inc(a_filled, 1)
                elif name == "v":
                    turn_a(name, j)
                    if j == 0:
                        pe.wait_ge(ld_v, 16)
                    src, w = (xT, w_attn[:, 2, :]) if is_local(j) else (ctxT, w_cross[:, WV, :])
                    for kt in range(NT):
                        at = b * S + kt * P
                        last = pe.matmul(ps_a[:, kt * D:(kt + 1) * D], src[:, at:at + P], w, start=True, stop=True)
                    last.then_inc(a_filled, 1)
                elif name == "nm_turn":
                    turn_a(name, j)
                    pe.wait_ge(nm_ready, j + 1)
                    for qt in range(NT):
                        last = pe.transpose(ps_a[0:NPART * H, :].bitcast(BF16)[:, qt * P:(qt + 1) * P],
                                            nm[:, qt].rearrange("p a h -> p (a h)"), ident_b[:, :])
                    last.then_inc(a_filled, 1)
                elif name in ("norm0", "norm1"):
                    turn_e(name, j)
                    qt = int(name[-1])
                    pe.wait_ge(o_out, 2 * j + 2)
                    for g in range(4):
                        last = pe.transpose(ps_e[:, g * P:(g + 1) * P], oT[:, g, qt * P:(qt + 1) * P], ident[:, :])
                    last.then_inc(e_filled, 1)
                elif name == "o_turn":
                    turn_e(name, j)
                    for qt in range(NT):
                        last = pe.transpose(ps_e[:, qt * P:(qt + 1) * P], o_tok[:, qt, :], ident[:, :])
                    last.then_inc(e_filled, 1)
                elif name == "proj":
                    turn_e(name, j)
                    w = w_attn[:, 3, :] if is_local(j) else w_cross[:, WO, :]
                    for qt in range(NT):
                        last = pe.matmul(ps_e[:, qt * D:(qt + 1) * D], oT_n[:, qt * P:(qt + 1) * P], w,
                                         start=True, stop=True)
                    last.then_inc(e_filled, 1)
                elif name == "y_turn":
                    turn_e(name, j)
                    pe.wait_ge(y_ready, j + 1)
                    y = y1 if is_local(j) else y2
                    for qt in range(NT):
                        last = pe.transpose(ps_e[:, qt * P:(qt + 1) * P], y[:, b * NT + qt, :], ident[:, :])
                    last.then_inc(e_filled, 1)
                elif name == "route":
                    turn_e(name, j)
                    pe.wait_ge(yT_ready, j + 1)
                    if j == B:
                        pe.wait_ge(ld_route, 32)
                    for qt in range(NT):
                        at = b * S + qt * P
                        last = pe.matmul(ps_e[:, qt * E:(qt + 1) * E], y2T[:, at:at + P], w_router[:, :],
                                         start=True, stop=True)
                    last.then_inc(e_filled, 1)
                elif name == "w_turn":
                    turn_e(name, j)
                    pe.wait_ge(w_ready, b + 1)
                    for qt in range(NT):
                        last = pe.transpose(ps_e[0:E, qt * P:(qt + 1) * P], w_full[:, qt, :], ident[:, :])
                    last.then_inc(e_filled, 1)

            def gate_up(m):
                c, e = m // NE, expert_order(m % NE)
                if m == 0:
                    pe.wait_ge(gu_split, 2 * NE // 2)
                    pe.wait_ge(max_ready, NJ * H)
                if m == EARLY:
                    pe.wait_ge(exp_done, NJ * H)
                if m % NE == 0:
                    pe.wait_ge(y2_split, c + 1)
                if bank_before(m) is not None:
                    pe.wait_ge(gu_read, bank_before(m) + 1)
                for k, dst in enumerate(gate_up_of(m)):
                    col = (2 * e + k) * F
                    for i, (w, y) in enumerate(((w_gu_hi, y2T_hi), (w_gu_hi, y2T_lo), (w_gu_lo, y2T_hi))):
                        last = pe.matmul(dst, w[:, col:col + F], y[:, c * CH:(c + 1) * CH],
                                         start=(i == 0), stop=(i == 2), skip_group_check=True)
                last.then_inc(gu_done, 1)

            def down(m):
                c, e = m // NE, expert_order(m % NE)
                pe.wait_ge(h_hi_ready, m + 1)
                if m == 0:
                    pe.wait_ge(down_split, 2 * NE // 2)
                    pe.wait_ge(nm_turned, NJ)
                if m in (NE, 2 * NE):
                    pe.wait_ge(o_out, 2 * NJ - 2 + m // NE)
                if m == 3 * NE:
                    pe.wait_ge(var3_ready, 1)
                for i, (w, h) in enumerate(((w_down_hi, h_hi), (w_down_lo, h_hi), (w_down_hi, h_lo))):
                    if h is h_lo:
                        pe.wait_ge(h_lo_ready, m + 1)
                    last = pe.matmul(down_out(c), w[:, e, :], h[:, m % H_RING, :],
                                     start=(m % NE == 0 and i == 0), stop=(m % NE == NE - 1 and i == 2),
                                     skip_group_check=True)
                last.then_inc(down_done, 1)

            def turn_down(c):
                pe.wait_ge(down_out_T, c + 1)
                for k in range(CT):
                    last = pe.transpose(down_out(c)[:, k * P:(k + 1) * P], downT[:, k * P:(k + 1) * P], ident[:, :])
                last.then_inc(down_turned, 1)

            def keep_warm(products):
                pe.wait_ge(masks_ready, 3)
                for _ in range(products):
                    pe.matmul(ps_t[0][:, 0:NT * BAND], ident_b[:, :], band[:, :], start=True, stop=True,
                              skip_group_check=True)

            for n in STEPS:
                if n == -AHEAD:
                    keep_warm(WARM)
                m = unit_at(n)
                if m is not None and m < NC * NE and n >= MOE0:
                    gate_up(m)
                if 0 <= n + AHEAD < MOE0:
                    first_scores((n + AHEAD) // H, (n + AHEAD) % H)
                if 0 <= n < MOE0:
                    second_scores(n // H, n % H)
                for name, j in tasks_at(n):
                    task(name, j)
                for g in range(4 * NJ):
                    if weigh_step(g) == n:
                        weigh_values(g // 4, g % 4)
                if m is not None and n < MOE0:
                    gate_up(m)
                if m is not None and DOWN_LAG <= m < NC * NE + DOWN_LAG:
                    down(m - DOWN_LAG)
                for c in range(NC):
                    if m == NE * (c + 1) + DOWN_LAG + 1:
                        turn_down(c)

        @block.vector
        def _(dve):
            chain = [0]

            def link(ins):
                chain[0] += 1
                ins.then_inc(dve_step, 1)
                dve.wait_ge(dve_step, chain[0])

            dve.memset(zero_rows(q_stack[0]), 0)
            dve.memset(zero_rows(k_stack[0]), 0).then_inc(rows_zero[0], 1)
            dve.wait_ge(a_filled, 1)
            dve.tensor_scalar(full[1][:, :], ps_o[0][:, 0:S], bias[:, BK:BK + 1], None,
                              ALU.add).then_inc(full_ready[1], 1)
            dve.wait_ge(full_ready[1], 1)
            dve.tensor_copy(parts[1][:, 0, :], full[1][:, :]).then_inc(hi_ready[1], 1)
            dve.wait_ge(hi_ready[1], 1)
            dve.tensor_tensor(rest[1][:, :], full[1][:, :], parts[1][:, 0, :], ALU.subtract).then_inc(rest_ready[1], 1)
            dve.wait_ge(rest_ready[1], 1)
            dve.tensor_copy(parts[1][:, 1, :], rest[1][:, :]).then_inc(mid_ready[1], 1)
            dve.wait_ge(mid_ready[1], 1)
            dve.tensor_tensor(parts[1][:, 2, :], rest[1][:, :], parts[1][:, 1, :],
                              ALU.subtract).then_inc(lo_ready[1], 1)
            for i in range(3):
                dve.memset(k_stack[i][NM0:KT_ROWS, :, :].bitcast(U32), 0x3F803F80).then_inc(ones_fixed, 1)

            def maxima(j, i):
                unit = H * j + i
                qt, pair = i // 8, i % 8
                width = q_cols(j, 0)[1]
                dve.wait_ge(s_scored, unit + 1)
                if i == 0 and j >= 2:
                    dve.wait_ge(nm_ready, j - 1)
                dve.tensor_reduce(row_max[j % 2][:, qt, 2 * pair:2 * pair + 2],
                                  ps_s[unit % 2][:, 0:2 * width].rearrange("p (k w) -> p k w", k=2),
                                  AX.X, ALU.max).then_inc(max_ready, 1)

            def rope_side(side, j):
                b0 = (XQ, XK)[side]
                if side == 1:
                    dve.wait_ge(a_filled, a_turn("k", j) + 1)
                else:
                    dve.wait_ge(a_filled, a_turn("q", j) + 1)
                if j > B:
                    dve.wait_ge(full_ready[side], turn_of(side, j - 1) + 1)
                if j == B:
                    dve.wait_ge(ld_cross, 64)
                dve.scalar_tensor_tensor(rope[side][:, 0, :], ps_a[:, 0:S], bias[:, b0:b0 + 1], cos_t[:, :],
                                         ALU.add, ALU.mult)
                dve.scalar_tensor_tensor(rope[side][:, 1, :], ps_a[:, S:2 * S], bias[:, b0 + 1:b0 + 2], sin_t[:, :],
                                         ALU.add, ALU.mult).then_inc(roped[side], 1)

            def layer_norm_stats(src, st, mv, ve, tiles, ready):
                for k in range(tiles):
                    last = dve.bn_stats(st[:, k, :], src[:, k, :])
                link(last)
                for k in range(tiles):
                    last = dve.bn_aggr(mv[:, k, :], st[:, k, :])
                link(last)
                dve.tensor_scalar(ve[:, :], mv[:, :, 1], EPS, None, ALU.add).then_inc(ready, 1)

            def task(name, j):
                b = j % B
                if name == "q" and not is_local(j):
                    rope_side(0, j)
                if name == "k":
                    rope_side(1, j)
                if name == "neg_max":
                    dve.wait_ge(max_ready, H * (j + 1))
                    if j >= 1:
                        dve.wait_ge(a_filled, a_turn("nm_turn", j - 1) + 1)
                    m = row_max[j % 2]
                    link(dve.tensor_scalar(nm[:, :, 0, :], m[:, :, :], -1.0, None, ALU.mult))
                    link(dve.scalar_tensor_tensor(nm_rest[:, 0], m[:, :, :], -1.0, nm[:, :, 0, :],
                                                  ALU.mult, ALU.subtract))
                    link(dve.tensor_copy(nm[:, :, 1, :], nm_rest[:, 0]))
                    dve.tensor_tensor(nm[:, :, 2, :], nm_rest[:, 0], nm[:, :, 1, :],
                                      ALU.subtract).then_inc(nm_ready, 1)
                if name in ("norm0", "norm1"):
                    qt = int(name[-1])
                    dve.wait_ge(e_filled, e_turn(name, j) + 1)
                    o = ps_e[:, :].rearrange("p (h c) -> p h c", c=VW)
                    link(dve.reciprocal(denom[:, :], o[:, :, HD]))
                    ins = dve.tensor_tensor(o_tok[:, qt, :].rearrange("p (h c) -> p h c", c=HD), o[:, :, 0:HD],
                                            denom[:, :].unsqueeze(2).to_broadcast([P, H, HD]), ALU.mult)
                    ins.then_inc(o_norm, 1)
                if name == "proj":
                    dve.wait_ge(e_filled, e_turn(name, j) + 1)
                    if is_local(j):
                        dve.wait_ge(res_ready, 1)
                        res = x_tok
                    else:
                        dve.wait_ge(y1_res_ready, b + 1)
                        res = y1_res
                    ins = dve.tensor_tensor(z[:, :, :].rearrange("p n d -> p (n d)"), ps_e[:, 0:NT * D],
                                            res[:, b * NT:(b + 1) * NT, :].rearrange("p n d -> p (n d)"), ALU.add)
                    ins.then_inc(z_ready, 1)
                    dve.wait_ge(z_ready, j + 1)
                    layer_norm_stats(z, stats, mean_var, var_eps, NT, var_ready)
                if name == "ln":
                    dve.wait_ge(rstd_ready, j + 1)
                    y = y1 if is_local(j) else y2
                    for k in range(NT):
                        last = dve.tensor_scalar(y[:, b * NT + k, :], z[:, k, :], mean_var[:, k, 0:1],
                                                 rstd[:, k:k + 1], ALU.subtract, ALU.mult)
                    last.then_inc(y_ready, 1)
                    dve.wait_ge(y_ready, j + 1)
                if name == "y_turn" and not is_local(j):
                    dve.wait_ge(yT_ready, j + 1)
                    dve.tensor_tensor(y2T_lo[:, tok(b)], ps_e[:, 0:S], y2T_hi[:, tok(b)].bitcast(F32),
                                      ALU.subtract).then_inc(y2_split, 1)
                if name == "route":
                    dve.wait_ge(e_filled, e_turn(name, j) + 1)
                    ins = dve.tensor_copy(logits[:, :, :].rearrange("p n e -> p (n e)"), ps_e[:, 0:NT * E])
                    ins.then_inc(logits_ready, 1)
                    dve.wait_ge(logits_ready, b + 1)
                    for k in range(NT):
                        last = dve.max(top[:, k, :], logits[:, k, :])
                    last.then_inc(top_ready, 1)
                    dve.wait_ge(top_ready, b + 1)
                    for k in range(NT):
                        last = dve.max_index(top_at[:, k, :], top[:, k, :], logits[:, k, :])
                    link(last)
                    link(dve.tensor_copy(top_f[:, :, :], top_at[:, :, :]))
                if name == "gates":
                    dve.wait_ge(gate_exp, b + 1)
                    link(dve.tensor_scalar(gate_s[:, :, :], gate_e[:, :, :], 1.0, None, ALU.add))
                    link(dve.reciprocal(gate_s[:, :, :], gate_s[:, :, :]))
                    for k in range(NT):
                        last = dve.tensor_scalar(pick[:, k, :], iota[:, :], top_f[:, k, 0:1], gate_s[:, k, 0:1],
                                                 ALU.is_equal, ALU.mult)
                    link(last)
                    if b >= 1:
                        dve.wait_ge(e_filled, e_turn("w_turn", j - 1) + 1)
                    for k in range(NT):
                        last = dve.tensor_scalar(w_full[:, k, :], iota[:, :], top_f[:, k, 1:2], gate_s[:, k, 1:2],
                                                 ALU.is_equal, ALU.mult)
                    link(last)
                    dve.tensor_tensor(w_full[:, :, :], w_full[:, :, :], pick[:, :, :], ALU.add).then_inc(w_ready, 1)

            def hidden(m):
                e = expert_order(m % NE)
                gate, up = gate_up_of(m)
                dve.wait_ge(silu_done, m + 1)
                if e >= E and m >= FULL_RING:
                    dve.wait_ge(h_lo_ready, m - FULL_RING + 1)
                if m >= 2 and routed(m - 1):
                    dve.wait_ge(h_ready, routed(m - 1))
                dst = h_raw[:, m % 2, :] if e < E else h_full[:, m % FULL_RING, :]
                if unit_step(m) > TANH_LAST:
                    ins = dve.tensor_tensor(dst, silu[:, m % 2, :], up, ALU.mult)
                else:
                    link(dve.scalar_tensor_tensor(silu[:, m % 2, :], silu[:, m % 2, :], 1.0, gate,
                                                  ALU.add, ALU.mult))
                    ins = dve.scalar_tensor_tensor(dst, silu[:, m % 2, :], 0.5, up, ALU.mult, ALU.mult)
                ins.then_inc(gu_read, 1)

            def low_part(m):
                if m == LOW_BY_POOL and m:
                    dve.wait_ge(h_lo_ready, m)
                dve.wait_ge(h_hi_ready, m + 1)
                if m >= H_RING:
                    dve.wait_ge(down_done, m - H_RING + 1)
                dve.tensor_tensor(h_lo[:, m % H_RING, :], h_full[:, m % FULL_RING, :],
                                  h_hi[:, m % H_RING, :].bitcast(F32), ALU.subtract).then_inc(h_lo_ready, 1)

            def last_norm_stats(c):
                dve.wait_ge(down_turned, c + 1)
                if c:
                    dve.wait_ge(y3_ready, c)
                link(dve.tensor_tensor(z3[:, :, :].rearrange("p n d -> p (n d)"), down_out(c),
                                       y2[:, CT * c:CT * (c + 1), :].rearrange("p n d -> p (n d)"), ALU.add))
                layer_norm_stats(z3, stats3, mean_var3, var_eps3, CT, var3_ready)

            def last_norm(c):
                dve.wait_ge(rstd3_ready, c + 1)
                if c:
                    dve.wait_ge(stored, 16 * c)
                for k in range(CT):
                    last = dve.tensor_scalar(y3[:, k, :], z3[:, k, :], mean_var3[:, k, 0:1], rstd3[:, k:k + 1],
                                             ALU.subtract, ALU.mult)
                last.then_inc(y3_ready, 1)

            for n in STEPS:
                if 0 <= n + AHEAD < MOE0:
                    maxima((n + AHEAD) // H, (n + AHEAD) % H)
                for name, j in tasks_at(n, "dve"):
                    task(name, j)
                m = unit_at(n)
                if m is not None and m < NC * NE:
                    hidden(m)
                if m is not None and LOW_BY_POOL + LO_LAG <= m < NC * NE + LO_LAG:
                    low_part(m - LO_LAG)
                for c in range(NC):
                    if m == NE * (c + 1) + DOWN_LAG + 1:
                        last_norm_stats(c)
                    if m == NE * (c + 1) + DOWN_LAG + 2:
                        last_norm(c)

        @block.scalar
        def _(act):
            def exponentials(j, h):
                unit = H * j + h
                width = NT * q_cols(j, 0)[1]
                act.wait_ge(t_scored, unit + 1)
                if unit >= PT_RING:
                    act.wait_ge(pv_done, (unit - PT_RING) // 4 + 1)
                act.activation(probs[:, unit % PT_RING, 0:width], ps_t[unit % 2][:, 0:width], ACT.Exp,
                               scale=SCALE).then_inc(exp_done, 1)

            def hi_part(side, j):
                k = turn_of(side, j)
                act.wait_ge(full_ready[side], k + 1)
                if k:
                    act.wait_ge(scr_written[side], 16 * k)
                act.activation(parts[side][:, 0, :], full[side][:, :], ACT.Copy).then_inc(hi_ready[side], 1)

            def mid_part(side, j):
                act.wait_ge(rest_ready[side], turn_of(side, j) + 1)
                act.activation(parts[side][:, 1, :], rest[side][:, :], ACT.Copy).then_inc(mid_ready[side], 1)

            def task(name, j):
                b = j % B
                if name == "q" and is_local(j):
                    act.wait_ge(a_filled, a_turn(name, j) + 1)
                    for side in ((0, 1) if j else (0,)):
                        if j:
                            act.wait_ge(rest_ready[side], turn_of(side, j))
                        ins = act.activation(full[side][:, :], ps_a[:, side * S:(side + 1) * S], ACT.Identity,
                                             bias=bias[:, BQ + side:BQ + side + 1])
                        ins.then_inc(full_ready[side], 1)
                if name == "q_hi":
                    for side in sides_with_q(j):
                        hi_part(side, j)
                if name == "k_hi":
                    hi_part(1, j)
                if name == "q_mid":
                    for side in sides_with_q(j):
                        mid_part(side, j)
                if name == "k_mid":
                    mid_part(1, j)
                if name == "v":
                    act.wait_ge(a_filled, a_turn(name, j) + 1)
                    if j < 3:
                        act.wait_ge(cols_fixed, j + 1)
                    else:
                        act.wait_ge(pv_done, 4 * (j - 2))
                    act.activation(v_ones[j % 3][:, :, :, 0:HD],
                                   ps_a[:, 0:NT * D].rearrange("p (n h c) -> p n h c", n=NT, c=HD),
                                   ACT.Copy).then_inc(v_ready, 1)
                if name == "nm_turn":
                    act.wait_ge(a_filled, a_turn(name, j) + 1)
                    if j:
                        act.wait_ge(nm_stacked[(j - 1) % 2], 16 * ((j - 1) // 2 + 1))
                    act.activation(nm_t[:, :], ps_a[0:NPART * H, :].bitcast(BF16)[:, 0:S],
                                   ACT.Copy).then_inc(nm_turned, 1)
                    act.wait_ge(nm_turned, j + 1)
                    if j >= 3:
                        act.wait_ge(t_scored, H * (j - 2))
                    act.dma_start(q_stack[j % 3][NM0:KT_ROWS, :, :], nm_t[:, :]).then_inc(nm_stacked[j % 2], 16)
                if name in ("o_even", "o_odd"):
                    k = int(name == "o_odd")
                    act.wait_ge(pv_done, 4 * j + 2 * k + 2)
                    if j and k == 0:
                        act.wait_ge(e_filled, e_turn("norm1", j - 1) + 1)
                    act.activation(oT[:, 2 * k:2 * k + 2, :].rearrange("p g s -> p (g s)"), ps_o[k][:, :],
                                   ACT.Copy).then_inc(o_out, 1)
                if name == "o_turn":
                    act.wait_ge(e_filled, e_turn(name, j) + 1)
                    col = BV if is_local(j) else XV
                    act.activation(oT_n[:, :], ps_e[:, 0:S], ACT.Identity,
                                   bias=bias[:, col:col + 1]).then_inc(o_turned, 1)
                if name == "y_turn":
                    act.wait_ge(e_filled, e_turn(name, j) + 1)
                    if is_local(j):
                        act.activation(y1T[:, tok(b)], ps_e[:, 0:S], ACT.Copy).then_inc(yT_ready, 1)
                    else:
                        act.activation(y2T[:, tok(b)], ps_e[:, 0:S], ACT.Copy)
                        act.activation(y2T_hi[:, tok(b)], ps_e[:, 0:S], ACT.Copy).then_inc(yT_ready, 1)
                if name == "route":
                    act.wait_ge(top_ready, b + 1)
                    act.activation(gate_e[:, :, :], top[:, :, 0:TOP_K], ACT.Exp, scale=-1.0).then_inc(gate_exp, 1)
                if name == "w_turn":
                    act.wait_ge(e_filled, e_turn(name, j) + 1)
                    if b:
                        act.wait_ge(w_scr, 16 * b)
                    act.activation(wT[:, :], ps_e[0:E, 0:S], ACT.Copy).then_inc(wT_ready, 1)
                    act.wait_ge(wT_ready, b + 1)
                    act.dma_start(scratch_w[:, tok(b)], wT[:]).then_inc(w_scr, 16)

            def high_part(m):
                if expert_order(m % NE) < E:
                    act.wait_ge(h_ready, routed(m) + 1)
                else:
                    act.wait_ge(gu_read, m + 1)
                if m >= H_RING:
                    act.wait_ge(down_done, m - H_RING + 1)
                act.activation(h_hi[:, m % H_RING, :], h_full[:, m % FULL_RING, :],
                               ACT.Copy).then_inc(h_hi_ready, 1)

            def gate(m):
                act.wait_ge(gu_done, m + 1)
                if m == 0:
                    act.wait_ge(t_scored, H * (NJ - 2))
                if m >= 2:
                    act.wait_ge(gu_read, m - 1)
                if unit_step(m) > TANH_LAST:
                    act.activation(silu[:, m % 2, :], gate_up_of(m)[0], ACT.Silu).then_inc(silu_done, 1)
                else:
                    act.activation(silu[:, m % 2, :], gate_up_of(m)[0], ACT.Tanh, scale=0.5).then_inc(silu_done, 1)

            for n in STEPS:
                if n == -16:
                    act.memzero(zero_rows(q_stack[2]))
                    act.memzero(zero_rows(k_stack[2])).then_inc(rows_zero[2], 1)
                if 0 <= n < MOE0:
                    exponentials(n // H, n % H)
                for name, j in tasks_at(n, "act"):
                    task(name, j)
                m = unit_at(n)
                if m is not None and m < NC * NE:
                    gate(m)
                if m is not None and HI_LAG <= m < NC * NE + HI_LAG:
                    high_part(m - HI_LAG)
                for c in range(NC):
                    if m == NE * (c + 1) + DOWN_LAG:
                        act.wait_ge(down_done, NE * (c + 1))
                        if c:
                            act.wait_ge(down_turned, c)
                        act.activation(downT, down_out(c), ACT.Copy).then_inc(down_out_T, 1)

        @block.gpsimd
        def _(pool):
            for m in (ident_b, ident):
                pool.memset(m[:], 0.0).then_inc(pool_step, 1)
            pool.memset(band[:], 0.0).then_inc(pool_step, 1)
            pool.wait_ge(pool_step, 3)
            for m in (ident_b, ident):
                pool.affine_select(out=m[:], in_=m[:], compare_op=ALU.not_equal, fill=1.0, base=0,
                                   pattern=[[-1, P]], channel_multiplier=1).then_inc(masks_ready, 1)
            for k in range(NT):
                cols = band[:, k * BAND:(k + 1) * BAND]
                pool.affine_select(out=cols, in_=cols, compare_op=ALU.is_ge, fill=MASKED, base=HALF * (k + 1),
                                   pattern=[[-1, BAND]], channel_multiplier=1).then_inc(pool_step, 1)
            pool.wait_ge(pool_step, 5)
            for k in range(NT):
                cols = band[:, k * BAND:(k + 1) * BAND]
                last = pool.affine_select(out=cols, in_=cols, compare_op=ALU.is_ge, fill=MASKED,
                                          base=HALF * (1 - k), pattern=[[1, BAND]], channel_multiplier=-1)
            last.then_inc(masks_ready, 1)
            pool.memset(half_neg[:], -0.5)
            pool.memset(half_neg3[:], -0.5).then_inc(pool_step, 1)
            pool.wait_ge(pool_step, 6)
            pool.memset(zero_rows(q_stack[1]), 0).then_inc(pool_step, 1)
            pool.memset(zero_rows(k_stack[1]), 0).then_inc(rows_zero[1], 1)
            pool.wait_ge(pool_step, 7)
            pool.wait_ge(rows_zero[1], 1)

            def fix_columns(i):
                pool.memset(v_ones[i][:, :, :, HD + 1:VW], 0.0)
                pool.memset(v_ones[i][:, :, :, HD:HD + 1], 1.0).then_inc(cols_fixed, 1)

            def split(side, j):
                k = turn_of(side, j)
                pool.wait_ge(hi_ready[side], k + 1)
                if k:
                    pool.wait_ge(lo_ready[side], k)
                    pool.wait_ge(mid_ready[side], k)
                pool.tensor_tensor(rest[side][:, :], full[side][:, :], parts[side][:, 0, :],
                                   ALU.subtract).then_inc(rest_ready[side], 1)

            def lo_part(side, j):
                pool.wait_ge(mid_ready[side], turn_of(side, j) + 1)
                pool.wait_ge(rest_ready[side], turn_of(side, j) + 1)
                pool.tensor_tensor(parts[side][:, 2, :], rest[side][:, :], parts[side][:, 1, :],
                                   ALU.subtract).then_inc(lo_ready[side], 1)

            def sum_rope(side, j):
                pool.wait_ge(roped[side], j - B + 1)
                pool.wait_ge(rest_ready[side], turn_of(side, j))
                pool.tensor_tensor(full[side][:, :], rope[side][:, 0, :], rope[side][:, 1, :],
                                   ALU.add).then_inc(full_ready[side], 1)

            def task(name, j):
                b = j % B
                if name == "q" and not is_local(j):
                    sum_rope(0, j)
                if name == "k":
                    sum_rope(1, j)
                if name == "q_hi":
                    for side in sides_with_q(j):
                        split(side, j)
                if name == "k_hi":
                    split(1, j)
                if name == "q_mid":
                    for side in sides_with_q(j):
                        lo_part(side, j)
                if name == "k_mid":
                    lo_part(1, j)
                if name == "proj":
                    pool.wait_ge(var_ready, j + 1)
                    if j:
                        pool.wait_ge(y_ready, j)
                    pool.tensor_tensor(rstd[:, :], var_eps[:, :], half_neg[:, :], ALU.pow).then_inc(rstd_ready, 1)
                if name == "y_turn" and is_local(j):
                    pool.wait_ge(y_ready, j + 1)
                    pool.tensor_tensor(y1_res[:, b * NT:(b + 1) * NT, :], y1[:, b * NT:(b + 1) * NT, :],
                                       out_bias[:, 1, :].unsqueeze(1).to_broadcast([P, NT, D]),
                                       ALU.add).then_inc(y1_res_ready, 1)

            def split_weights(k):
                cols = slice(k * GU_CH, (k + 1) * GU_CH)
                pool.wait_ge(ld_gu[k % 2], 32 * (k // 2 + 1))
                pool.tensor_scalar(w_gu_hi[:, cols], w_gu[:, k % 2, :], 1.0, 0.0, ALU.mult,
                                   ALU.add).then_inc(gu_split, 1)
                two = slice(2 * k, 2 * k + 2)
                pool.tensor_scalar(w_down_hi[:, two, :], w_down[:, k % 2], 1.0, 0.0, ALU.mult,
                                   ALU.add).then_inc(down_split, 1)
                pool.wait_ge(gu_split, 2 * k + 1)
                pool.tensor_tensor(w_gu_lo[:, cols], w_gu[:, k % 2, :], w_gu_hi[:, cols].bitcast(F32),
                                   ALU.subtract).then_inc(gu_split, 1)
                pool.wait_ge(down_split, 2 * k + 1)
                pool.tensor_tensor(w_down_lo[:, two, :], w_down[:, k % 2], w_down_hi[:, two, :].bitcast(F32),
                                   ALU.subtract).then_inc(down_split, 1)

            def keep_band(pair):
                if not pool_bands(pair):
                    return
                pool.wait_ge(exp_done, 2 * pair + 2)
                at = 2 * pair % PT_RING
                for first, width, base, sign in ((0, HALF, HALF, 1), (HALF, P, 0, -1), (BAND, P, 0, 1),
                                                 (BAND + P, HALF, 0, -1)):
                    cols = probs[:, at:at + 2, first:first + width]
                    last = pool.affine_select(out=cols, in_=cols, compare_op=ALU.is_ge, fill=0.0, base=base,
                                              pattern=[[0, 2], [sign, width]], channel_multiplier=-sign)
                last.then_inc(banded, 1)

            def low_part(m):
                pool.wait_ge(h_hi_ready, m + 1)
                if m >= H_RING:
                    pool.wait_ge(down_done, m - H_RING + 1)
                pool.tensor_tensor(h_lo[:, m % H_RING, :], h_full[:, m % FULL_RING, :],
                                   h_hi[:, m % H_RING, :].bitcast(F32), ALU.subtract).then_inc(h_lo_ready, 1)

            def gated(m):
                if expert_order(m % NE) < E:
                    r = routed(m)
                    pool.wait_ge(gu_read, m + 1)
                    pool.wait_ge(w_bc_ready[r % W_RING], 16 * (r // W_RING + 1))
                    if m >= FULL_RING:
                        pool.wait_ge(h_lo_ready, m - FULL_RING + 1)
                    pool.tensor_tensor(h_full[:, m % FULL_RING, :], h_raw[:, m % 2, :], w_bc[r % W_RING],
                                       ALU.mult).then_inc(h_ready, 1)

            for n in STEPS:
                if n in (-30, -18, -12):
                    fix_columns((-30, -18, -12).index(n))
                if n == -8:
                    pool.wait_ge(ld_tok, 48)
                    pool.tensor_tensor(x_tok[:, :, :], x_tok[:, :, :],
                                       out_bias[:, 0, :].unsqueeze(1).to_broadcast([P, B * NT, D]),
                                       ALU.add).then_inc(res_ready, 1)
                    pool.wait_ge(pool_step, 6)
                if n % 2 == BAND_LAG % 2 and 0 <= n - BAND_LAG < B * H:
                    keep_band((n - BAND_LAG) // 2)
                for name, j in tasks_at(n, "pool"):
                    task(name, j)
                for k in range(NE // 2):
                    if n == SPLIT0 + SPLIT_STEP * k:
                        split_weights(k)
                m = unit_at(n)
                if m is not None and m < NC * NE:
                    gated(m)
                if m is not None and LO_LAG <= m < LOW_BY_POOL + LO_LAG:
                    low_part(m - LO_LAG)
                for c in range(NC):
                    if unit_at(n) == NE * (c + 1) + DOWN_LAG + 1:
                        pool.wait_ge(var3_ready, c + 1)
                        if c:
                            pool.wait_ge(y3_ready, c)
                        pool.tensor_tensor(rstd3[:, :], var_eps3[:, :], half_neg3[:, :],
                                           ALU.pow).then_inc(rstd3_ready, 1)


def _layouts(inp):
    c = np.ascontiguousarray

    def by_dim(w):
        return w.reshape(w.shape[:-1] + (H, HD)).swapaxes(-1, -2).reshape(w.shape)

    def swap_halves(w):
        s = w.shape
        return by_dim(w.reshape(s[:-1] + (H, 2, HD // 2))[..., ::-1, :].reshape(s))

    x = inp["x"].reshape(N_TOK, D)
    wq, wk, wv, wo = (inp[f"L0_xattn_W{n}"].T for n in "qkvo")
    bq, bk, bv = (inp[f"L0_xattn_b{n}"] for n in "qkv")
    bqkv = inp["L0_attn_b_qkv"]
    wqkv = inp["L0_attn_w_qkv"].reshape(D, 3, D)
    gu = np.concatenate([
        inp["L0_ffn_gate_up_w"].transpose(1, 0, 2).reshape(D, E * 2 * F),
        np.stack([inp["L0_ffn_shared_gate_w"].reshape(NSH, F, D), inp["L0_ffn_shared_up_w"].reshape(NSH, F, D)],
                 axis=1).transpose(3, 0, 1, 2).reshape(D, NSH * 2 * F)], axis=1)
    down = np.concatenate([
        inp["L0_ffn_down_w"].transpose(1, 0, 2),
        inp["L0_ffn_shared_down_w"].T.reshape(NSH, F, D).transpose(1, 0, 2)], axis=1)
    return {
        "x": c(x), "xT": c(x.T), "ctxT": c(inp["ctx_1024"].reshape(N_TOK, D).T),
        "w_attn": c(np.stack([by_dim(wqkv[:, 0]), by_dim(wqkv[:, 1]), wqkv[:, 2], inp["L0_attn_w_out"]], axis=1)),
        "w_cross": c(np.stack([by_dim(wq), swap_halves(wq), by_dim(wk), swap_halves(wk), wv, wo], axis=1)),
        "bias": c(np.stack([by_dim(bqkv[0:D]), by_dim(bqkv[D:2 * D]), bqkv[2 * D:], by_dim(bq), swap_halves(bq),
                            by_dim(bk), swap_halves(bk), bv], axis=1)),
        "out_bias": c(np.stack([inp["L0_attn_b_out"], inp["L0_xattn_bo"]])),
        "w_router": c(inp["L0_ffn_router_w"].T), "w_gu": c(gu), "w_down": c(down),
    }


def _tables():
    inv_freq = (1.0 / 10000.0 ** (np.arange(0, HD, 2, dtype=np.float32) / np.float32(HD))).astype(np.float32)
    angle = np.arange(S, dtype=np.float32)[None, :] * inv_freq[:, None]
    cos, sin = np.cos(angle).astype(np.float32), np.sin(angle).astype(np.float32)
    return {
        "cos": np.repeat(np.concatenate([cos, cos]), H, axis=0),
        "sin": np.repeat(np.concatenate([-sin, sin]), H, axis=0),
        "iota": np.tile(np.arange(E, dtype=np.float32), (P, 1)),
    }


def kernel(**inputs):
    import concourse.bacc as _bacc
    from concourse import mybir as _mybir
    from concourse.bass_utils import run_bass_kernel_spmd as _run

    arrays = {**_layouts({k: np.asarray(v) for k, v in inputs.items()}), **_tables()}
    nc = _bacc.Bacc("TRN2", target_bir_lowering=False, num_devices=1)
    t = {n: nc.dram_tensor(n + "_dram", a.shape, _mybir.dt.from_np(a.dtype), kind="ExternalInput").ap()
         for n, a in arrays.items()}
    scratch_parts = nc.dram_tensor("scratch_parts", [NJ, 2, NPART, P, S], _mybir.dt.bfloat16).ap()
    scratch_w = nc.dram_tensor("scratch_w", [E, N_TOK], _mybir.dt.float32).ap()
    out = nc.dram_tensor("out_dram", [N_TOK, D], _mybir.dt.float32, kind="ExternalOutput").ap()
    decoder_layer(nc, t, scratch_parts, scratch_w, out)
    r = _run(nc, [{n + "_dram": a for n, a in arrays.items()}], core_ids=[0])
    return r.results[0]["out_dram"].reshape(B, S, D)
```
